# Optimizing a Trainium2 kernel written in Bass

```python
import numpy as np
import jax
import jax.numpy as jnp

def _softmax(x, axis=-1):
    return jax.nn.softmax(x, axis=axis)

def _gelu(x):
    return jax.nn.gelu(x, approximate=True)

def _silu(x):
    return jax.nn.silu(x)

def _sigmoid(x):
    return jax.nn.sigmoid(x)

def _layernorm(x, axis=-1, eps=1e-05):
    m = jnp.mean(x, axis=axis, keepdims=True)
    v = jnp.var(x, axis=axis, keepdims=True)
    return (x - m) / jnp.sqrt(v + eps)

def _scatter_add(tgt, idx, src, axis=0):
    return tgt.at[idx].add(src)

def _segment_sum(src, seg, n):
    return jax.ops.segment_sum(src, seg, n)
kernel_name = 'mk_xattn_ffn_d2_seqx_r4_99bfd0'

def setup_inputs(seed: int=0):
    np.random.seed(seed)
    _w = jnp.asarray

    def _rec_inputs():
        import jax
        import jax.numpy as jnp
        _rk = jax.random.key(seed)
        x = -0.0003929 + 0.9999 * jax.random.normal(jax.random.fold_in(_rk, 1), (8, 256, 256), jnp.float32)
        _lenS = 256 - jax.random.randint(jax.random.fold_in(_rk, 7), (8,), 0, max(1, 256 // 4) + 1, jnp.int32)
        _lenS2 = 256 - jax.random.randint(jax.random.fold_in(_rk, 8), (8,), 0, max(1, 256 // 4) + 1, jnp.int32)
        _ctx_1024P = jax.random.normal(jax.random.fold_in(_rk, 11), (8, 16, 256), jnp.float32)
        _ctx_1024c = jax.random.dirichlet(jax.random.fold_in(_rk, 511), 0.3 * jnp.ones((16,), jnp.float32), (8, 256))
        _ctx_1024t = jnp.einsum('bsk,bkd->bsd', _ctx_1024c, _ctx_1024P)
        _ctx_1024t = _ctx_1024t * jax.lax.rsqrt(jnp.mean(jnp.square(_ctx_1024t)) + 1e-12) * 0.953939
        ctx_1024 = 2.81802e-05 + 1.00001 * (_ctx_1024t + 0.3 * jax.random.normal(jax.random.fold_in(_rk, 611), (8, 256, 256), jnp.float32))
        return (x, ctx_1024)
    x, ctx_1024 = _rec_inputs()

    def _L0_xattn_setup():
        import jax, jax.numpy as jnp
        import numpy as np
        D_MODEL = 256
        NHEAD = 16
        WINDOW = 128
        key = jax.random.key(seed)
        ks = jax.random.split(key, 7)
        B, L, D = (4, 1024, D_MODEL)
        s = 0.02
        return {'q': jax.random.normal(ks[0], (B, L, D), jnp.float32), 'k': jax.random.normal(ks[1], (B, L, D), jnp.float32), 'v': jax.random.normal(ks[2], (B, L, D), jnp.float32), 'in_proj_w': jax.random.normal(ks[3], (3 * D, D), jnp.float32) * s, 'in_proj_b': jnp.zeros((3 * D,), jnp.float32), 'out_w': jax.random.normal(ks[4], (D, D), jnp.float32) * s, 'out_b': jnp.zeros((D,), jnp.float32)}
    _L0_xattn_all = _L0_xattn_setup()
    _L0_xattn_in = {k: v for k, v in _L0_xattn_all.items() if k in ('in_proj_w', 'in_proj_b', 'out_w', 'out_b')}
    del _L0_xattn_all

    def _L0_ffn_setup():
        import jax, jax.numpy as jnp
        import numpy as np
        D_MODEL = 256
        N_EXPERTS = 16
        TOP_K = 2
        EXPERT_DIM = 256
        SHARED_DIM = 512
        B, T = (2, 256)
        key = jax.random.key(seed)
        ks = jax.random.split(key, 7)
        std = 0.02
        return {'x': jax.random.normal(ks[0], (B, T, D_MODEL), dtype=jnp.float32), 'router_w': jax.random.normal(ks[1], (N_EXPERTS, D_MODEL), dtype=jnp.float32) * std, 'gate_up_w': jax.random.normal(ks[2], (N_EXPERTS, D_MODEL, 2 * EXPERT_DIM), dtype=jnp.float32) * std, 'down_w': jax.random.normal(ks[3], (N_EXPERTS, EXPERT_DIM, D_MODEL), dtype=jnp.float32) * std, 'shared_gate_w': jax.random.normal(ks[4], (SHARED_DIM, D_MODEL), dtype=jnp.float32) * std, 'shared_up_w': jax.random.normal(ks[5], (SHARED_DIM, D_MODEL), dtype=jnp.float32) * std, 'shared_down_w': jax.random.normal(ks[6], (D_MODEL, SHARED_DIM), dtype=jnp.float32) * std}
    _L0_ffn_all = _L0_ffn_setup()
    _L0_ffn_in = {k: v for k, v in _L0_ffn_all.items() if k in ('router_w', 'gate_up_w', 'down_w', 'shared_gate_w', 'shared_up_w', 'shared_down_w')}
    del _L0_ffn_all

    def _L1_xattn_setup():
        import jax, jax.numpy as jnp
        import numpy as np
        D_MODEL = 256
        N_HEADS = 16
        HEAD_DIM = D_MODEL // N_HEADS
        key = jax.random.key(seed)
        ks = jax.random.split(key, 10)
        B, Lq, Lkv = (4, 128, 512)
        s = 1.0 / np.sqrt(D_MODEL)
        return {'q': jax.random.normal(ks[0], (B, Lq, D_MODEL), jnp.float32), 'kv': jax.random.normal(ks[1], (B, Lkv, D_MODEL), jnp.float32), 'Wq': jax.random.normal(ks[2], (D_MODEL, D_MODEL), jnp.float32) * s, 'bq': jnp.zeros((D_MODEL,), jnp.float32), 'Wk': jax.random.normal(ks[3], (D_MODEL, D_MODEL), jnp.float32) * s, 'bk': jnp.zeros((D_MODEL,), jnp.float32), 'Wv': jax.random.normal(ks[4], (D_MODEL, D_MODEL), jnp.float32) * s, 'bv': jnp.zeros((D_MODEL,), jnp.float32), 'Wo': jax.random.normal(ks[5], (D_MODEL, D_MODEL), jnp.float32) * s, 'bo': jnp.zeros((D_MODEL,), jnp.float32)}
    _L1_xattn_all = _L1_xattn_setup()
    _L1_xattn_in = {k: v for k, v in _L1_xattn_all.items() if k in ('Wq', 'bq', 'Wk', 'bk', 'Wv', 'bv', 'Wo', 'bo')}
    del _L1_xattn_all

    def _L1_ffn_setup():
        import jax, jax.numpy as jnp
        import numpy as np
        N_EMBD = 256
        NUM_EXPERTS = 8
        TOP_K = 2
        D_FF = 4 * N_EMBD
        B, S = (4, 512)
        key = jax.random.key(seed)
        ks = jax.random.split(key, 7)
        scale = lambda fan_in: 1.0 / np.sqrt(fan_in)
        x = jax.random.normal(ks[0], (B, S, N_EMBD), dtype=jnp.float32)
        W_router = jax.random.normal(ks[1], (N_EMBD, NUM_EXPERTS), dtype=jnp.float32) * scale(N_EMBD)
        b_router = jnp.zeros((NUM_EXPERTS,), dtype=jnp.float32)
        W1 = jax.random.normal(ks[2], (NUM_EXPERTS, N_EMBD, D_FF), dtype=jnp.float32) * scale(N_EMBD)
        b1 = jnp.zeros((NUM_EXPERTS, D_FF), dtype=jnp.float32)
        W2 = jax.random.normal(ks[3], (NUM_EXPERTS, D_FF, N_EMBD), dtype=jnp.float32) * scale(D_FF)
        b2 = jnpp = jnp.zeros((NUM_EXPERTS, N_EMBD), dtype=jnp.float32)
        return {'x': x, 'W_router': W_router, 'b_router': b_router, 'W1': W1, 'b1': b1, 'W2': W2, 'b2': b2}
    _L1_ffn_all = _L1_ffn_setup()
    _L1_ffn_in = {k: v for k, v in _L1_ffn_all.items() if k in ('W_router', 'b_router', 'W1', 'b1', 'W2', 'b2')}
    del _L1_ffn_all
    return {'x': x, 'ctx_1024': ctx_1024, 'L0_xattn_in_proj_w': _L0_xattn_in['in_proj_w'], 'L0_xattn_in_proj_b': _L0_xattn_in['in_proj_b'], 'L0_xattn_out_w': _L0_xattn_in['out_w'], 'L0_xattn_out_b': _L0_xattn_in['out_b'], 'L0_ffn_router_w': _L0_ffn_in['router_w'], 'L0_ffn_gate_up_w': _L0_ffn_in['gate_up_w'], 'L0_ffn_down_w': _L0_ffn_in['down_w'], 'L0_ffn_shared_gate_w': _L0_ffn_in['shared_gate_w'], 'L0_ffn_shared_up_w': _L0_ffn_in['shared_up_w'], 'L0_ffn_shared_down_w': _L0_ffn_in['shared_down_w'], 'L1_xattn_Wq': _L1_xattn_in['Wq'], 'L1_xattn_bq': _L1_xattn_in['bq'], 'L1_xattn_Wk': _L1_xattn_in['Wk'], 'L1_xattn_bk': _L1_xattn_in['bk'], 'L1_xattn_Wv': _L1_xattn_in['Wv'], 'L1_xattn_bv': _L1_xattn_in['bv'], 'L1_xattn_Wo': _L1_xattn_in['Wo'], 'L1_xattn_bo': _L1_xattn_in['bo'], 'L1_ffn_W_router': _L1_ffn_in['W_router'], 'L1_ffn_b_router': _L1_ffn_in['b_router'], 'L1_ffn_W1': _L1_ffn_in['W1'], 'L1_ffn_b1': _L1_ffn_in['b1'], 'L1_ffn_W2': _L1_ffn_in['W2'], 'L1_ffn_b2': _L1_ffn_in['b2']}

def reference(x, ctx_1024, L0_xattn_in_proj_w, L0_xattn_in_proj_b, L0_xattn_out_w, L0_xattn_out_b, L0_ffn_router_w, L0_ffn_gate_up_w, L0_ffn_down_w, L0_ffn_shared_gate_w, L0_ffn_shared_up_w, L0_ffn_shared_down_w, L1_xattn_Wq, L1_xattn_bq, L1_xattn_Wk, L1_xattn_bk, L1_xattn_Wv, L1_xattn_bv, L1_xattn_Wo, L1_xattn_bo, L1_ffn_W_router, L1_ffn_b_router, L1_ffn_W1, L1_ffn_b1, L1_ffn_W2, L1_ffn_b2):
    import jax
    import jax.numpy as jnp

    def _L0_xattn_ref(q, k, v, in_proj_w, in_proj_b, out_w, out_b):
        import jax, jax.numpy as jnp
        import numpy as np
        D_MODEL = 256
        NHEAD = 16
        WINDOW = 128
        B, L, D = q.shape
        H, W = (NHEAD, WINDOW)
        hd = D // H
        nW = L // W
        Wq, Wk, Wv = (in_proj_w[:D], in_proj_w[D:2 * D], in_proj_w[2 * D:])
        bq, bk, bv = (in_proj_b[:D], in_proj_b[D:2 * D], in_proj_b[2 * D:])
        qp = (q @ Wq.T + bq).reshape(B, nW, W, H, hd)
        kp = (k @ Wk.T + bk).reshape(B, nW, W, H, hd)
        vp = (v @ Wv.T + bv).reshape(B, nW, W, H, hd)
        scale = 1.0 / np.sqrt(hd).astype(np.float32)
        scores = jnp.einsum('bnqhd,bnkhd->bnhqk', qp, kp) * scale
        attn = jax.nn.softmax(scores, axis=-1)
        out = jnp.einsum('bnhqk,bnkhd->bnqhd', attn, vp).reshape(B, L, D)
        return out @ out_w.T + out_b

    def _L0_ffn_ref(x, router_w, gate_up_w, down_w, shared_gate_w, shared_up_w, shared_down_w):
        import jax, jax.numpy as jnp
        import numpy as np
        D_MODEL = 256
        N_EXPERTS = 16
        TOP_K = 2
        EXPERT_DIM = 256
        SHARED_DIM = 512
        B, T = (2, 256)
        Bb, Tt, C = x.shape
        N = Bb * Tt
        E = gate_up_w.shape[0]
        logits = jnp.einsum('btc,ec->bte', x, router_w)
        top_vals, top_idx = jax.lax.top_k(logits, TOP_K)
        gates = jax.nn.sigmoid(top_vals)
        xf = x.reshape(N, C)
        sel = top_idx.reshape(N, TOP_K)
        gw = gates.reshape(N, TOP_K)
        w_full = jnp.zeros((N, E), dtype=x.dtype).at[jnp.arange(N)[:, None], sel].add(gw)
        gu = jnp.einsum('nc,ech->neh', xf, gate_up_w)
        gate, up = jnp.split(gu, 2, axis=-1)
        h = jax.nn.silu(gate) * up
        out_all = jnp.einsum('neh,ehc->nec', h, down_w)
        moe = jnp.einsum('ne,nec->nc', w_full, out_all).reshape(Bb, Tt, C)
        sg = jnp.einsum('btc,sc->bts', x, shared_gate_w)
        su = jnp.einsum('btc,sc->bts', x, shared_up_w)
        shared = jnp.einsum('bts,cs->btc', jax.nn.silu(sg) * su, shared_down_w)
        return moe + shared

    def _L1_xattn_ref(q, kv, Wq, bq, Wk, bk, Wv, bv, Wo, bo):
        import jax, jax.numpy as jnp
        import numpy as np
        D_MODEL = 256
        N_HEADS = 16
        HEAD_DIM = D_MODEL // N_HEADS
        B, Lq, _ = q.shape
        Lkv = kv.shape[1]
        qh = (q @ Wq.T + bq).reshape(B, Lq, N_HEADS, HEAD_DIM)
        kh = (kv @ Wk.T + bk).reshape(B, Lkv, N_HEADS, HEAD_DIM)
        vh = (kv @ Wv.T + bv).reshape(B, Lkv, N_HEADS, HEAD_DIM)
        scale = 1.0 / np.sqrt(HEAD_DIM).astype(np.float32)
        scores = jnp.einsum('bqhd,bkhd->bhqk', qh, kh) * scale
        attn = jax.nn.softmax(scores, axis=-1)
        ctx = jnp.einsum('bhqk,bkhd->bqhd', attn, vh).reshape(B, Lq, D_MODEL)
        out = ctx @ Wo.T + bo
        return out

    def _L1_ffn_ref(x, W_router, b_router, W1, b1, W2, b2):
        import jax, jax.numpy as jnp
        import numpy as np
        N_EMBD = 256
        NUM_EXPERTS = 8
        TOP_K = 2
        D_FF = 4 * N_EMBD
        B, S = (4, 512)
        Bv, Sv, D = x.shape
        flat_x = x.reshape(-1, D)
        T = flat_x.shape[0]
        logits = flat_x @ W_router + b_router
        top_vals, top_idx = jax.lax.top_k(logits, TOP_K)
        neg_inf = jnp.full_like(logits, -jnp.inf)
        sparse_logits = neg_inf.at[jnp.arange(T)[:, None], top_idx].set(top_vals)
        router_weights = jax.nn.softmax(sparse_logits, axis=-1)
        final_output = jnp.zeros_like(flat_x)
        for e in range(NUM_EXPERTS):
            expert_mask = jnp.any(top_idx == e, axis=-1)
            h = jax.nn.relu(flat_x @ W1[e] + b1[e])
            y = h @ W2[e] + b2[e]
            w = router_weights[:, e] * expert_mask.astype(x.dtype)
            final_output = final_output + y * w[:, None]
        return final_output.reshape(Bv, Sv, D)
    x = x + _L0_xattn_ref(_layernorm(x, axis=-1), ctx_1024, ctx_1024, L0_xattn_in_proj_w, L0_xattn_in_proj_b, L0_xattn_out_w, L0_xattn_out_b)
    x = x + _L0_ffn_ref(_layernorm(x, axis=-1), L0_ffn_router_w, L0_ffn_gate_up_w, L0_ffn_down_w, L0_ffn_shared_gate_w, L0_ffn_shared_up_w, L0_ffn_shared_down_w)
    x = x + _L1_xattn_ref(_layernorm(x, axis=-1), ctx_1024, L1_xattn_Wq, L1_xattn_bq, L1_xattn_Wk, L1_xattn_bk, L1_xattn_Wv, L1_xattn_bv, L1_xattn_Wo, L1_xattn_bo)
    x = x + _L1_ffn_ref(_layernorm(x, axis=-1), L1_ffn_W_router, L1_ffn_b_router, L1_ffn_W1, L1_ffn_b1, L1_ffn_W2, L1_ffn_b2)
    return x

_drawn_inputs = setup_inputs


def setup_inputs(seed=0):
    import zlib

    import numpy as np

    out = dict(_drawn_inputs(seed))
    spreads = {'L0_xattn_in_proj_b': (0.0, 0.1),
     'L0_xattn_out_b': (0.0, 0.1),
     'L1_xattn_bq': (0.0, 0.1),
     'L1_xattn_bk': (0.0, 0.1),
     'L1_xattn_bv': (0.0, 0.1),
     'L1_xattn_bo': (0.0, 0.1),
     'L1_ffn_b_router': (0.0, 0.1),
     'L1_ffn_b1': (0.0, 0.1),
     'L1_ffn_b2': (0.0, 0.1)}
    factors = {}
    for name, (base, spread) in spreads.items():
        noise = np.random.default_rng([zlib.crc32(name.encode()), seed]).standard_normal(out[name].shape)
        drawn = base * np.exp(spread * noise) if base else spread * noise
        out[name] = jnp.asarray(drawn.astype(out[name].dtype))
    for name, factor in factors.items():
        out[name] = (out[name] * factor).astype(out[name].dtype)
    return out
```

```python
from contextlib import ExitStack

import concourse.bass as bass
from concourse import mybir


def xattn_moe_program(nc, a, out):
    F32, BF16, U32, I32 = mybir.dt.float32, mybir.dt.bfloat16, mybir.dt.uint32, mybir.dt.int32
    ALU, ACT, AX = mybir.AluOpType, mybir.ActivationFunctionType, mybir.AxisListType
    ds = bass.ds

    P = 128
    N, D = a["x"].shape
    T = N // P
    KD = D // P
    TC = 4
    CW = TC * P
    NC = T // TC
    H, HD = 16, 16
    HB = P // HD
    PARTS = 3
    QK = [(0, 0), (0, 1), (1, 0), (1, 1), (0, 2), (2, 0)]
    KR = len(QK) * HD
    SCALE = float(HD) ** -0.5
    EPS = 1e-5
    V1 = HD + 1
    KV = [1, 2]
    NE = [16, 8]
    NS = [48, 39]
    GROUPS = 2
    RING = 3
    SH = 512
    SHB = SH // P
    UPW = [512, 1024]
    HK = [2, 8]
    assert all(s * P >= 2 * N + (e - 1) * (P - 1) and s % RING == 0 for s, e in zip(NS, NE))
    STEPS = lambda n: [1 << i for i in range((n - 1).bit_length())]

    ctx = ExitStack()
    with ctx:
        def sb(name, shape, dt=F32):
            return ctx.enter_context(nc.sbuf_tensor(name, shape, dt))

        def sem(name):
            return ctx.enter_context(nc.semaphore(name))

        def dram(name, shape, dt):
            return nc.dram_tensor(name, shape, dt, kind="Internal").ap()

        q_parts_d = [dram(f"q_parts_d{l}", (NC, P, PARTS, KD, CW), BF16) for l in range(2)]
        k_parts_d = [dram(f"k_parts_d{l}", (NC, P, PARTS, KD, CW), BF16) for l in range(2)]
        slot_in = dram("slot_in", (NS[0] * P, D), F32)
        slot_out = [dram(f"slot_out{l}", (NS[l] * P, D), F32) for l in range(2)]

        x_res = sb("x_res", [P, T, D])
        consts = sb("consts", list(a["consts"].shape))
        ident, ltri, ones = consts[:, 0:P], consts[:, P:2 * P], consts[:, 2 * P:3 * P]
        iota_e = consts[:, 3 * P:3 * P + 16]
        iota_c = consts[:, 3 * P + 16:3 * P + 32]
        iota_s = consts[:, 3 * P + 32:3 * P + 32 + 48]

        arena1 = sb("arena1", [P, 24576])
        k_stack = arena1[:, 0:16384].bitcast(BF16).rearrange("p (h t) -> p h t", h=H)
        q_stack = arena1[:, 16384:24576].bitcast(BF16).rearrange("p (h t) -> p h t", h=H)
        QRING = 2 * CW
        WSZ = [KD * UPW[l] + HK[l] * D for l in range(2)]
        w_up = [[arena1[:, r * 4096:r * 4096 + KD * UPW[l]].rearrange("p (k n) -> p k n", k=KD)
                 for r in range(RING)] for l in range(2)]
        w_dn = [[arena1[:, r * 4096 + KD * UPW[l]:r * 4096 + WSZ[l]].rearrange("p (k n) -> p k n", k=HK[l])
                 for r in range(RING)] for l in range(2)]
        xn_all = arena1[:, 12288:12288 + T * D].rearrange("p (t d) -> p t d", t=T)
        y_got = arena1[:, 12288:12288 + 2 * T * D].rearrange("p (t s d) -> p t s d", t=T, s=2)
        sh_gate = arena1[:, 20480:21504].rearrange("p (k n) -> p k n", k=KD)
        sh_up = arena1[:, 21504:22528].rearrange("p (k n) -> p k n", k=KD)
        sh_down = arena1[:, 22528:23552].rearrange("p (k n) -> p k n", k=SHB)

        arena2 = sb("arena2", [P, 4096])
        qf = arena2[:, 0:1024].rearrange("p (m t) -> p m t", m=KD)
        kf = arena2[:, 1024:2048].rearrange("p (m t) -> p m t", m=KD)
        rest = arena2[:, 2048:3072].rearrange("p (m t) -> p m t", m=KD)
        probs = [arena2[:, 1024 * i:1024 * (i + 1)] for i in range(4)]
        sh_hid = [arena2[:, 2048 * u:2048 * (u + 1)].rearrange("p (m t) -> p m t", m=SHB) for u in range(2)]

        arena3 = sb("arena3", [P, T * H * V1])
        v_all = arena3[:, :].rearrange("p (t h c) -> p t h c", t=T, h=H)
        xnT_all = arena3[:, 0:KD * N].rearrange("p (k t) -> p k t", k=KD)

        arena4 = sb("arena4", [P, 5632])
        ctxT = [arena4[:, 1024 * u:1024 * (u + 1)].rearrange("p (k t) -> p k t", k=KD) for u in range(2)]
        q_parts = arena4[:, 2048:3584].bitcast(BF16).rearrange("p (s m t) -> p s m t", s=PARTS, m=KD)
        k_parts = arena4[:, 3584:5120].bitcast(BF16).rearrange("p (s m t) -> p s m t", s=PARTS, m=KD)
        rows = [arena4[:, 256 * u:256 * (u + 1)] for u in range(RING)]
        rowsT = [arena4[:, 768 + 256 * u:768 + 256 * (u + 1)].rearrange("p (k t) -> p k t", k=KD) for u in range(RING)]
        hid = arena4[:, 1536:2560]
        hidT = arena4[:, 2560:3584].rearrange("p (k t) -> p k t", k=8)
        y_rows = [arena4[:, 3584 + 256 * u:3584 + 256 * (u + 1)] for u in range(RING)]
        b2_row = [arena4[:, 4352 + 256 * u:4352 + 256 * (u + 1)] for u in range(RING)]
        b1_col = [arena4[:, 5120 + 8 * u:5120 + 8 * (u + 1)] for u in range(RING)]
        gate_act = arena4[:, 5376:5632]
        zeros = arena4[:, 5120:5632]

        xn = [sb(f"xn{u}", [P, TC, D]) for u in range(2)]
        xnT = [sb(f"xnT{u}", [P, KD, CW]) for u in range(2)]
        att_w = sb("att_w", [P, 4, KD, D])
        wq, wk, wv, wo = (att_w[:, i] for i in range(4))
        bqk = sb("bqk", [P, 2, KD])
        bvo = sb("bvo", [P, 2, D])
        router_w = sb("router_w", [P, KD, 16])
        router_b = sb("router_b", [P, 16])
        v_tile = [sb(f"v_tile{u}", [P, 2, H, V1]) for u in range(2)]
        stats = sb("stats", [P, TC, 6])
        mean_var = sb("mean_var", [P, TC, 2])
        var_eps, std, rstd = (sb(n, [P, TC]) for n in ("var_eps", "std", "rstd"))
        neg_max = [sb(f"neg_max{u}", [P, H]) for u in range(2)]
        neg_maxT = sb("neg_maxT", [H, P], BF16)
        att_raw = sb("att_raw", [P, 512])
        inv_den = sb("inv_den", [P, H, 1])
        att = sb("att", [P, D])
        attT = sb("attT", [P, KD, P])
        logits = sb("logits", [P, T, 16])
        top = sb("top", [P, T, 8])
        top_i = sb("top_i", [P, T, 8], U32)
        idx_f = sb("idx_f", [P, 2, T, 1])
        hot1, hot2, hot, cnt, run0, run1 = (arena4[:, 2560 + 256 * i:2560 + 256 * (i + 1)] for i in range(6))
        over = arena4[:, 4096:4352].rearrange("p (e c) -> p e c", c=16)
        tiles_e, end0, end1, base = (sb(n, [P, 16]) for n in ("tiles_e", "end0", "end1", "base"))
        slot_f = sb("slot_f", [P, 2, T])
        slot = sb("slot", [P, 2, T], I32)
        le = arena4[:, 4352:5120].rearrange("p (s e) -> p s e", e=16)
        exp_f = sb("exp_f", [P, 48])
        expert = sb("expert", [P, 48], I32)
        gates = sb("gates", [P, T, 2])
        gap = sb("gap", [P, T])

        bank = ctx.enter_context(nc.psum_tensor("bank", [P, 8, 512], F32))
        trT = bank[:, 0:2]
        kP, vP, qP = bank[:, 2:4], bank[:, 4:6], bank[:, 6:8]
        mx = [bank[:, 0], bank[:, 1]]
        sc = [bank[:, 2:4], bank[:, 4:6]]
        attP, misc = bank[:, 6], bank[:, 7]
        rP = [bank[:, 2], bank[:, 3]]
        posP, cntP = bank[:, 4], bank[:, 5]
        sgP, suP = [bank[:, 0], bank[:, 1]], [bank[:, 2], bank[:, 3]]
        sdP = bank[:, 6:8]
        upP, hidTP, yP, rowsTP = bank[:, 0:2], bank[:, 2:4], bank[:, 4, 0:D], bank[:, 5]

        once = {n: sem(n) for n in ("x_in", "consts_in", "zeros_set", "slots_zeroed", "out_stored")}

        def block_sems(l):
            names = """w_in var_ready sd_ready xn_ready bo_added k_mm v_mm tr_mm q_mm kf_ready xT_ready qf_ready
                kparts_ready qparts_ready v_ready ones_set k_stored q_stored k_in q_in chunk_step
                max_mm max_read nmt_mm nm_ready shift_in sc_mm exp_done pv_mm raw_ready ott_mm norm_step
                norm_done at_mm atT_ready op_mm x_att
                r_mm lg_ready xn_kept
                step routed cnt_mm gates_ready scattered
                xt_mm rowsT_ready up_mm hid_a hid_v ht_mm hidT_a hidT_v dn_mm y_ready x_ffn""".split()
            s = {n: sem(f"{n}_{l}") for n in names}
            s["ctx_in"] = [sem(f"ctx_in{u}_{l}") for u in range(2)]
            s["v_in"] = [sem(f"v_in{u}_{l}") for u in range(2)]
            s["up_in"] = [sem(f"up_in{u}_{l}") for u in range(RING)]
            s["dn_in"] = [sem(f"dn_in{u}_{l}") for u in range(RING)]
            s["y_stored"] = [sem(f"y_stored{u}_{l}") for u in range(RING)]
            s["gathered"] = [sem(f"gathered{g}_{l}") for g in range(GROUPS)]
            return s

        B = [block_sems(l) for l in range(2)]
        sh = {n: sem(f"sh_{n}") for n in ("w_in", "xT_kept", "g_mm", "u_mm", "act", "hid", "d_mm", "x")}

        class Steps:
            def __init__(self, eng, s, start=0):
                self.eng, self.sem, self.start, self.n = eng, s, start, 0

            def then(self, ins):
                self.n += 1
                ins.then_inc(self.sem, 1)
                self.eng.wait_ge(self.sem, self.start + self.n)

        def after(eng, s, count):
            if not (isinstance(count, int) and count <= 0):
                eng.wait_ge(s, count)

        def in_pairs(eng, n, step):
            step(0, 0)
            step(1, 1)
            with eng.Fori(1, n // 2) as j:
                for u in range(2):
                    step(j * 2 + u, u)

        def in_rings(eng, n, step):
            for u in range(RING):
                step(u, u)
            with eng.Fori(1, n // RING - 1) as j:
                for u in range(RING):
                    step(j * RING + u, u)
            for u in range(RING):
                step(n - RING + u, u)

        def attend_in_pairs(eng, step):
            step(0, 0)
            step(1, 1)
            with eng.Fori(1, T // 2 - 1) as j:
                for u in range(2):
                    step(j * 2 + u, u)
            step(T - 2, 0)
            step(T - 1, 1)

        def least(x, top):
            return min(x, top) if isinstance(x, int) else x

        block = ctx.enter_context(nc.Block())

        @block.sync
        def _(sp):
            def load_attention_weights(l):
                s = B[l]
                if l:
                    sp.wait_ge(B[0]["x_att"], T)
                    sp.wait_ge(B[0]["lg_ready"], NC)
                sp.dma_start(att_w[:].rearrange("p w k n -> p (w k) n"),
                             a[f"att_w{l}"].rearrange("(q p) n -> p q n", p=P)).then_inc(s["w_in"], 16)
                sp.dma_start(bqk[:].rearrange("p b m -> p (b m)"), a[f"bqk{l}"]).then_inc(s["w_in"], 16)
                for i in range(2):
                    sp.dma_start(bvo[:, i], a[f"bvo{l}"][i:i + 1, :].to_broadcast([P, D])).then_inc(s["w_in"], 16)
                sp.dma_start(router_w[:, :, 0:NE[l]],
                             a[f"router_w{l}"].rearrange("(k p) e -> p k e", p=P)).then_inc(s["w_in"], 16)
                sp.dma_start(router_b[:, 0:NE[l]], a[f"router_b{l}"].to_broadcast([P, NE[l]])).then_inc(s["w_in"], 16)

            def store_parts(parts_d, c, parts, s_stored):
                sp.dma_start(parts_d[ds(c, 1)].rearrange("o p s m t -> p (o s m t)"),
                             parts.rearrange("p s m t -> p (s m t)")).then_inc(s_stored, 16)

            def stack(dst, parts_d, c, which, column, s_in):
                src = parts_d[ds(c, 1)].rearrange("o (h r) s m t -> r (o s m) h t", r=HD)
                for b, pair in enumerate(QK):
                    for m in range(KD):
                        sp.dma_start(dst[HD * b:HD * (b + 1), HB * m:HB * (m + 1), ds(column, CW)],
                                     src[:, pair[which] * KD + m]).then_inc(s_in, 16)

            def project(l):
                s = B[l]

                def step(c, u):
                    after(sp, s["v_mm"], c - 1)
                    sp.dma_start(ctxT[u], a["ctxT"].rearrange("(k p) t -> p k t", p=P)[:, :, ds(c * CW, CW)]).then_inc(s["ctx_in"][u], 16)
                    sp.wait_ge(s["kparts_ready"], c + 1)
                    store_parts(k_parts_d[l], c, k_parts, s["k_stored"])
                    sp.wait_ge(s["k_stored"], c * 16 + 16)
                    stack(k_stack, k_parts_d[l], c, 1, c * CW, s["k_in"])
                    sp.wait_ge(s["qparts_ready"], c + 1)
                    store_parts(q_parts_d[l], c, q_parts, s["q_stored"])
                    sp.wait_ge(s["q_stored"], c * 16 + 16)

                in_pairs(sp, NC, step)

            def attend(l):
                s = B[l]
                KW = KV[l]

                def load_queries(c):
                    if not (isinstance(c, int) and c < 2):
                        sp.wait_ge(s["sc_mm"], (c - 1) * TC * 2 * KW)
                    after(sp, s["q_in"], c * len(QK) * KD * 16)
                    stack(q_stack, q_parts_d[l], c, 0, (c % 2) * CW, s["q_in"])

                def load_values(i, u):
                    after(sp, s["pv_mm"], 2 * (i - 1))
                    first = i if KW == 1 else (i // 2) * 2
                    sp.dma_start(v_tile[u][:, 0:KW].rearrange("p k h c -> p (k h c)"),
                                 v_all[:, ds(first, KW)].rearrange("p k h c -> p (k h c)")).then_inc(s["v_in"][u], 16)

                def place_shift(i):
                    sp.wait_ge(s["nm_ready"], i + 1)
                    sp.dma_start(q_stack[KR:KR + 1, :, ds((i % (2 * TC)) * P, P)], neg_maxT[:]).then_inc(s["shift_in"], 16)

                load_queries(0)
                sp.wait_ge(s["v_ready"], NC)
                load_values(0, 0)
                place_shift(0)
                load_queries(1)

                def chunk(c, more):
                    for t in range(TC):
                        if more or t < TC - 1:
                            load_values(c * TC + t + 1, (t + 1) % 2)
                            place_shift(c * TC + t + 1)
                    if more is True:
                        load_queries(c + 2)

                with sp.Fori(0, NC - 2) as c:
                    chunk(c, True)
                chunk(NC - 2, 1)
                chunk(NC - 1, 0)

            def route(l):
                s = B[l]
                sp.wait_ge(s["x_att"], T)
                if l == 0:
                    sp.dma_start(sh_gate, a["sh_gate"].rearrange("(k p) n -> p k n", p=P)).then_inc(sh["w_in"], 16)
                    sp.dma_start(sh_up, a["sh_up"].rearrange("(k p) n -> p k n", p=P)).then_inc(sh["w_in"], 16)
                    sp.dma_start(sh_down, a["sh_down"].rearrange("(k p) n -> p k n", p=P)).then_inc(sh["w_in"], 16)

                def step(c, u):
                    sp.wait_ge(s["xn_ready"], NC + c + 1)
                    sp.dma_start(xn_all[:, ds(c * TC, TC)].rearrange("p t d -> p (t d)"),
                                 xn[u][:].rearrange("p t d -> p (t d)")).then_inc(s["xn_kept"], 16)
                    sp.wait_ge(s["xn_kept"], c * 16 + 16)
                    if l == 0:
                        sp.wait_ge(s["xT_ready"], NC + c + 1)
                        sp.dma_start(xnT_all[:, :, ds(c * CW, CW)], xnT[u][:]).then_inc(sh["xT_kept"], 16)
                        sp.wait_ge(sh["xT_kept"], c * 16 + 16)

                in_pairs(sp, NC, step)

            def experts(l):
                s = B[l]
                KW, up, dn = HK[l], a[f"exp_up{l}"], a[f"exp_dn{l}"]
                sp.wait_ge(s["routed"], 3)
                sp.wait_ge(s["scattered"], 2 * T * 16)

                def step(i, u):
                    use = i // RING if isinstance(i, int) else None
                    e = sp.value_load(expert[0:1, ds(i, 1)], min_val=0, max_val=NE[l] - 1)
                    after(sp, s["up_mm"], i - 2)
                    sp.dma_start(w_up[l][u], up[ds(e, 1)].rearrange("o (k p) n -> p (o k) n", p=P)).then_inc(s["up_in"][u], 16)
                    sp.dma_start(rows[u], slot_in[ds(i * P, P), :]).then_inc(s["up_in"][u], 16)
                    after(sp, s["dn_mm"], i - 2)
                    if l == 1:
                        after(sp, s["y_ready"], i - 2)
                        sp.dma_start(b1_col[u], a["exp_b1"][ds(e, 1)].rearrange("o p k -> p (o k)")).then_inc(s["dn_in"][u], 16)
                        sp.dma_start(b2_row[u], a["exp_b2"][ds(e, 1)].to_broadcast([P, D])).then_inc(s["dn_in"][u], 16)
                    sp.dma_start(w_dn[l][u], dn[ds(e, 1)].rearrange("o (k p) n -> p (o k) n", p=P)).then_inc(s["dn_in"][u], 16)
                    if not (isinstance(i, int) and i < RING):
                        store_rows(i - RING, u)

                def store_rows(i, u):
                    sp.wait_ge(s["y_ready"], i + 1)
                    sp.dma_start(slot_out[l][ds(i * P, P), :], y_rows[u]).then_inc(s["y_stored"][u], 16)

                in_rings(sp, NS[l], step)
                for u in range(RING):
                    store_rows(NS[l] - RING + u, u)

            sp.dma_start(x_res[:], a["x"].rearrange("(t p) d -> p t d", p=P)).then_inc(once["x_in"], 16)
            sp.dma_start(consts[:], a["consts"]).then_inc(once["consts_in"], 16)
            for l in range(2):
                load_attention_weights(l)
                if l == 0:
                    sp.wait_ge(once["zeros_set"], 1)
                    sp.dma_start(slot_in.rearrange("(p r) d -> p (r d)", p=P).rearrange("p (r w) -> p r w", w=512),
                                 zeros.rearrange("p (o w) -> p o w", o=1).to_broadcast([P, NS[0] * D // 512, 512])).then_inc(once["slots_zeroed"], 16)
                else:
                    sp.wait_ge(B[0]["x_ffn"], T)
                project(l)
                attend(l)
                route(l)
                experts(l)
            sp.wait_ge(B[1]["x_ffn"], T)
            sp.dma_start(out.rearrange("(t p) d -> p t d", p=P), x_res[:]).then_inc(once["out_stored"], 16)
            sp.wait_ge(once["out_stored"], 16)

        @block.tensor
        def _(pe):
            mm, tr = nc.tensor.matmul, nc.tensor.transpose

            def project(l):
                s = B[l]
                pe.wait_ge(s["w_in"], 6 * 16)
                if l:
                    pe.wait_ge(B[0]["y_ready"], NS[0])

                def step(c, u):
                    pe.wait_ge(s["ctx_in"][u], (c // 2 + 1) * 16)
                    after(pe, s["kf_ready"], c)
                    for m in range(KD):
                        for k in range(KD):
                            last = mm(kP[:, m], wk[:, k, m * P:(m + 1) * P], ctxT[u][:, k], start=k == 0, stop=k == KD - 1)
                    last.then_inc(s["k_mm"], 1)
                    pe.wait_ge(s["xn_ready"], c + 1)
                    after(pe, s["xT_ready"], c)
                    for t in range(TC):
                        for k in range(KD):
                            last = tr(trT[:, k, t * P:(t + 1) * P], xn[u][:, t, k * P:(k + 1) * P], ident)
                    last.then_inc(s["tr_mm"], 1)
                    after(pe, s["v_ready"], c)
                    for t in range(TC):
                        for k in range(KD):
                            last = mm(vP[:, t // 2, (t % 2) * D:(t % 2 + 1) * D], ctxT[u][:, k, t * P:(t + 1) * P], wv[:, k],
                                      start=k == 0, stop=k == KD - 1)
                    last.then_inc(s["v_mm"], 1)
                    pe.wait_ge(s["xT_ready"], c + 1)
                    after(pe, s["qf_ready"], c)
                    for m in range(KD):
                        for k in range(KD):
                            last = mm(qP[:, m], wq[:, k, m * P:(m + 1) * P], xnT[u][:, k], start=k == 0, stop=k == KD - 1)
                    last.then_inc(s["q_mm"], 1)

                in_pairs(pe, NC, step)

            def attend(l):
                s = B[l]
                KW = KV[l]
                NM = 4 * KW
                HM = H // NM
                NP = 2 * KW
                keys = lambda i: i * P if KW == 1 else (i // 2) * (2 * P)

                def maxima(i, lo, hi):
                    if lo == 0:
                        pe.wait_ge(s["q_in"], (i // TC + 1) * len(QK) * KD * 16)
                    for m in range(lo, hi):
                        after(pe, s["max_read"], i * NM + m - 1)
                        for hh in range(HM):
                            h = m * HM + hh
                            last = mm(mx[m % 2][:, hh * KW * P:(hh + 1) * KW * P], q_stack[0:KR, h, ds((i % (2 * TC)) * P, P)],
                                      k_stack[0:KR, h, ds(keys(i), KW * P)], start=True, stop=True)
                        last.then_inc(s["max_mm"], 1)

                def turn_maxima(i, u):
                    pe.wait_ge(s["max_read"], (i + 1) * NM)
                    after(pe, s["norm_done"], i - 1)
                    after(pe, s["nm_ready"], i)
                    tr(misc[0:H, 0:P], neg_max[u][:], ident).then_inc(s["nmt_mm"], 1)

                def scores(i, p):
                    half, kv = p // KW, p % KW
                    if p == 0:
                        pe.wait_ge(s["shift_in"], (i + 1) * 16)
                    after(pe, s["exp_done"], i * NP + p - 1)
                    for hh in range(8):
                        h = half * 8 + hh
                        last = mm(sc[p % 2][:, hh // 4, (hh % 4) * P:(hh % 4 + 1) * P], k_stack[0:KR + 1, h, ds(keys(i) + kv * P, P)],
                                  q_stack[0:KR + 1, h, ds((i % (2 * TC)) * P, P)], start=True, stop=True)
                    last.then_inc(s["sc_mm"], 1)

                def values(i, u, half):
                    if half == 0:
                        pe.wait_ge(s["v_in"][u], (i // 2 + 1) * 16)
                        after(pe, s["raw_ready"], i)
                    pe.wait_ge(s["exp_done"], i * NP + (half + 1) * KW)
                    for hh in range(8):
                        h = half * 8 + hh
                        j, g = h % 4, h // 4
                        for kv in range(KW):
                            pr = probs[2 * u + half] if KW == 1 else probs[half * KW + kv]
                            last = mm(attP[32 * j:32 * j + V1, g * P:(g + 1) * P], v_tile[u][:, kv, h], pr[:, hh * P:(hh + 1) * P],
                                      start=kv == 0, stop=kv == KW - 1)
                    last.then_inc(s["pv_mm"], 1)

                def turn_back(i):
                    pe.wait_ge(s["raw_ready"], i + 1)
                    after(pe, s["x_att"], i)
                    after(pe, s["nm_ready"], least(i + 2, T))
                    for g in range(4):
                        last = tr(misc[:, g * P:(g + 1) * P], att_raw[:, g * P:(g + 1) * P], ident)
                    last.then_inc(s["ott_mm"], 1)

                def turn_attention(i):
                    pe.wait_ge(s["norm_done"], i + 1)
                    pe.wait_ge(s["nm_ready"], least(i + 3, T))
                    for k in range(KD):
                        last = tr(misc[:, k * P:(k + 1) * P], att[:, k * P:(k + 1) * P], ident)
                    last.then_inc(s["at_mm"], 1)

                def project_out(i):
                    pe.wait_ge(s["atT_ready"], i + 1)
                    for k in range(KD):
                        last = mm(misc[:, 0:D], attT[:, k], wo[:, k], start=k == 0, stop=k == KD - 1)
                    last.then_inc(s["op_mm"], 1)

                def step(i, u):
                    first, final = isinstance(i, int) and i == 0, isinstance(i, int) and i == T - 1
                    for p in range(NP):
                        scores(i, p)
                        if not final:
                            maxima(i + 1, 2 * p, 2 * p + 2)
                        if p == 0 and not first:
                            turn_back(i - 1)
                    values(i, u, 0)
                    if not final:
                        turn_maxima(i + 1, 1 - u)
                    if not first:
                        turn_attention(i - 1)
                    values(i, u, 1)
                    if not first:
                        project_out(i - 1)

                pe.wait_ge(s["k_in"], NC * len(QK) * KD * 16)
                pe.wait_ge(s["ones_set"], 2)
                pe.wait_ge(s["xT_ready"], NC)
                pe.wait_ge(s["kf_ready"], NC)
                pe.wait_ge(s["v_ready"], NC)
                pe.wait_ge(s["qf_ready"], NC)
                pe.wait_ge(s["v_ready"], NC + 1)
                maxima(0, 0, NM)
                turn_maxima(0, 0)
                attend_in_pairs(pe, step)
                turn_back(T - 1)
                turn_attention(T - 1)
                project_out(T - 1)

            def route(l):
                s, E = B[l], NE[l]

                def step(c, u):
                    pe.wait_ge(s["xn_ready"], NC + c + 1)
                    pe.wait_ge(s["xT_ready"], NC + c)
                    for t in range(TC):
                        for k in range(KD):
                            last = tr(trT[:, k, t * P:(t + 1) * P], xn[u][:, t, k * P:(k + 1) * P], ident)
                    last.then_inc(s["tr_mm"], 1)
                    pe.wait_ge(s["xT_ready"], NC + c + 1)
                    after(pe, s["lg_ready"], c - 1)
                    for t in range(TC):
                        for k in range(KD):
                            last = mm(rP[u][:, t * E:(t + 1) * E], xnT[u][:, k, t * P:(t + 1) * P], router_w[:, k, 0:E],
                                      start=k == 0, stop=k == KD - 1)
                    last.then_inc(s["r_mm"], 1)

                in_pairs(pe, NC, step)

            def dispatch(l):
                s, E = B[l], NE[l]
                pe.wait_ge(s["routed"], 2)
                mm(posP[:, 0:T * E], ltri, hot[:, 0:T * E], start=True, stop=True)
                mm(cntP[:, 0:T * E], ones, hot[:, 0:T * E], start=True, stop=True).then_inc(s["cnt_mm"], 1)

            def shared():
                s = B[0]
                pe.wait_ge(sh["w_in"], 3 * 16)
                pe.wait_ge(sh["xT_kept"], NC * 16)
                pe.wait_ge(s["lg_ready"], NC)
                pe.wait_ge(s["xT_ready"], 2 * NC)

                def step(c, u):
                    for m in range(SHB):
                        after(pe, sh["hid"], c * SHB + m - 1)
                        for k in range(KD):
                            last = mm(sgP[m % 2], sh_gate[:, k, m * P:(m + 1) * P], xnT_all[:, k, ds(c * CW, CW)], start=k == 0, stop=k == KD - 1)
                        last.then_inc(sh["g_mm"], 1)
                        for k in range(KD):
                            last = mm(suP[m % 2], sh_up[:, k, m * P:(m + 1) * P], xnT_all[:, k, ds(c * CW, CW)], start=k == 0, stop=k == KD - 1)
                        last.then_inc(sh["u_mm"], 1)
                    pe.wait_ge(sh["hid"], (c + 1) * SHB)
                    after(pe, sh["x"], c)
                    for t in range(TC):
                        for k in range(SHB):
                            last = mm(sdP[:, t // 2, (t % 2) * D:(t % 2 + 1) * D], sh_hid[u][:, k, t * P:(t + 1) * P], sh_down[:, k],
                                      start=k == 0, stop=k == SHB - 1)
                    last.then_inc(sh["d_mm"], 1)

                in_pairs(pe, NC, step)

            def experts(l):
                s, S = B[l], NS[l]
                n_up, KW = UPW[l] // 512, HK[l]
                if l == 0:
                    pe.wait_ge(sh["hid"], NC * SHB)
                    pe.wait_ge(sh["x"], NC)
                else:
                    pe.wait_ge(s["xT_ready"], 2 * NC)
                    pe.wait_ge(s["lg_ready"], NC)
                pe.wait_ge(s["routed"], 3)

                def turn_rows(i, u):
                    pe.wait_ge(s["up_in"][u], (i // RING + 1) * 32)
                    after(pe, s["rowsT_ready"], i)
                    for k in range(KD):
                        last = tr(rowsTP[:, k * P:(k + 1) * P], rows[u][:, k * P:(k + 1) * P], ident)
                    last.then_inc(s["xt_mm"], 1)

                def first_product(i, u):
                    pe.wait_ge(s["rowsT_ready"], i + 1)
                    pe.wait_ge(s["up_in"][u], (i // RING + 1) * 32)
                    after(pe, s["hid_v"], i)
                    if l == 1:
                        after(pe, s["hid_a"], i)
                    for n in range(n_up):
                        for k in range(KD):
                            last = mm(upP[:, n], rowsT[u][:, k], w_up[l][u][:, k, n * 512:(n + 1) * 512], start=k == 0, stop=k == KD - 1)
                    last.then_inc(s["up_mm"], 1)

                def turn_hidden(i):
                    pe.wait_ge(s["hid_v"], i + 1)
                    if l == 1:
                        pe.wait_ge(s["hid_a"], i + 1)
                        after(pe, s["hidT_v"], i)
                    after(pe, s["hidT_a"], i)
                    for k in range(KW):
                        last = tr(hidTP[:, k // 4, (k % 4) * P:(k % 4 + 1) * P], hid[:, k * P:(k + 1) * P], ident)
                        if k == KW // 2 - 1 and l == 1:
                            last.then_inc(s["ht_mm"], 1)
                    last.then_inc(s["ht_mm"], 1)

                def second_product(i, u):
                    pe.wait_ge(s["hidT_a"], i + 1)
                    if l == 1:
                        pe.wait_ge(s["hidT_v"], i + 1)
                    pe.wait_ge(s["dn_in"][u], (i // RING + 1) * 16 * (3 if l else 1))
                    after(pe, s["y_ready"], i)
                    for k in range(KW):
                        last = mm(yP, hidT[:, k], w_dn[l][u][:, k], start=k == 0, stop=k == KW - 1)
                    last.then_inc(s["dn_mm"], 1)

                def step(i, u):
                    left = S - 1 - i if isinstance(i, int) else S
                    turn_hidden(i)
                    if left > 0:
                        first_product(i + 1, (u + 1) % RING)
                    second_product(i, u)
                    if left > 1:
                        turn_rows(i + 2, (u + 2) % RING)

                turn_rows(0, 0)
                first_product(0, 0)
                turn_rows(1, 1)
                in_rings(pe, S, step)

            pe.wait_ge(once["consts_in"], 16)
            for l in range(2):
                project(l)
                attend(l)
                route(l)
                dispatch(l)
                if l == 0:
                    shared()
                experts(l)

        @block.scalar
        def _(act):
            fn = nc.scalar.activation

            def project(l):
                s = B[l]

                def step(c, u):
                    act.wait_ge(s["var_ready"], c + 1)
                    fn(std[:], var_eps[:], ACT.Sqrt).then_inc(s["sd_ready"], 1)
                    act.wait_ge(s["k_mm"], c + 1)
                    after(act, s["kparts_ready"], c)
                    for m in range(KD):
                        last = fn(kf[:, m], kP[:, m], ACT.Identity, bias=bqk[:, 1, m:m + 1])
                    last.then_inc(s["kf_ready"], 1)
                    act.wait_ge(s["tr_mm"], c + 1)
                    after(act, s["q_mm"], c - 1)
                    fn(xnT[u][:], trT, ACT.Copy).then_inc(s["xT_ready"], 1)
                    act.wait_ge(s["q_mm"], c + 1)
                    after(act, s["qparts_ready"], c)
                    for m in range(KD):
                        last = fn(qf[:, m], qP[:, m], ACT.Identity, bias=bqk[:, 0, m:m + 1])
                    last.then_inc(s["qf_ready"], 1)

                in_pairs(act, NC, step)

            def attend(l):
                s = B[l]
                KW = KV[l]
                NP = 2 * KW

                def step(i, u):
                    first = isinstance(i, int) and i == 0
                    for p in range(NP):
                        half = p // KW
                        act.wait_ge(s["sc_mm"], i * NP + p + 1)
                        if KW == 1:
                            after(act, s["pv_mm"], 2 * (i - 2) + half + 1)
                            dst = probs[2 * u + half]
                        else:
                            after(act, s["pv_mm"], 2 * (i - 1) + half + 1)
                            dst = probs[p]
                        fn(dst.rearrange("p (b w) -> p b w", b=2), sc[p % 2], ACT.Exp, scale=SCALE).then_inc(s["exp_done"], 1)
                    if not first:
                        copy_attention(i - 1)
                    act.wait_ge(s["pv_mm"], 2 * (i + 1))
                    after(act, s["ott_mm"], i)
                    fn(att_raw[:], attP, ACT.Copy).then_inc(s["raw_ready"], 1)

                def copy_attention(i):
                    act.wait_ge(s["at_mm"], i + 1)
                    after(act, s["op_mm"], i)
                    fn(attT[:].rearrange("p k t -> p (k t)"), misc[:, 0:D], ACT.Copy).then_inc(s["atT_ready"], 1)

                act.wait_ge(s["kparts_ready"], NC)
                act.wait_ge(s["qparts_ready"], NC)
                attend_in_pairs(act, step)
                copy_attention(T - 1)

            def route(l):
                s = B[l]

                def step(c, u):
                    act.wait_ge(s["var_ready"], NC + c + 1)
                    fn(std[:], var_eps[:], ACT.Sqrt).then_inc(s["sd_ready"], 1)
                    act.wait_ge(s["tr_mm"], NC + c + 1)
                    after(act, s["r_mm"], c - 1)
                    if l == 0:
                        after(act, sh["xT_kept"], (c - 1) * 16)
                    fn(xnT[u][:], trT, ACT.Copy).then_inc(s["xT_ready"], 1)

                in_pairs(act, NC, step)

            def make_gates(l):
                s = B[l]
                act.wait_ge(s["routed"], 1)
                if l == 0:
                    fn(gates[:], top[:, :, 0:2], ACT.Sigmoid).then_inc(s["gates_ready"], 1)
                else:
                    fn(gap[:], gap[:], ACT.Exp).then_inc(s["gates_ready"], 1)

            def shared():
                def step(c, u):
                    for m in range(SHB):
                        act.wait_ge(sh["g_mm"], c * SHB + m + 1)
                        after(act, sh["hid"], c * SHB + m - 1)
                        fn(hid[:, (m % 2) * 512:(m % 2 + 1) * 512], sgP[m % 2], ACT.Silu).then_inc(sh["act"], 1)

                in_pairs(act, NC, step)

            def experts0():
                s = B[0]
                act.wait_ge(sh["hid"], NC * SHB)

                def step(i, u):
                    act.wait_ge(s["up_mm"], i + 1)
                    after(act, s["hid_v"], i)
                    fn(gate_act, upP[:, 0, 0:D], ACT.Silu).then_inc(s["hid_a"], 1)
                    act.wait_ge(s["ht_mm"], i + 1)
                    after(act, s["dn_mm"], i)
                    fn(hidT[:, 0:KD].rearrange("p k t -> p (k t)"), hidTP[:, 0, 0:D], ACT.Copy).then_inc(s["hidT_a"], 1)

                in_rings(act, NS[0], step)

            def experts1():
                s = B[1]

                def step(i, u):
                    act.wait_ge(s["up_mm"], i + 1)
                    after(act, s["ht_mm"], 2 * i)
                    fn(hid[:, 0:512], upP[:, 0], ACT.Copy).then_inc(s["hid_a"], 1)
                    act.wait_ge(s["ht_mm"], 2 * i + 1)
                    act.wait_ge(s["dn_in"][u], (i // RING + 1) * 48)
                    after(act, s["dn_mm"], i)
                    for k in range(4):
                        last = fn(hidT[:, k], hidTP[:, 0, k * P:(k + 1) * P], ACT.Relu, bias=b1_col[u][:, k:k + 1])
                    last.then_inc(s["hidT_a"], 1)

                in_rings(act, NS[1], step)

            act.wait_ge(B[0]["w_in"], 6 * 16)
            for l in range(2):
                if l:
                    act.wait_ge(B[1]["w_in"], 6 * 16)
                project(l)
                attend(l)
                route(l)
                make_gates(l)
                if l == 0:
                    shared()
                    experts0()
                else:
                    experts1()

        @block.vector
        def _(dve):
            v = nc.vector
            own = [Steps(dve, B[l]["step"]) for l in range(2)]

            def normalise(l, c, u, chain, n, free):
                for t in range(TC):
                    last = v.bn_stats(stats[:, t], x_res[:, ds(c * TC + t, 1)].rearrange("p o d -> p (o d)"))
                chain.then(last)
                for t in range(TC):
                    last = v.bn_aggr(mean_var[:, t], stats[:, t])
                chain.then(last)
                v.tensor_scalar(var_eps[:], mean_var[:, :, 1], EPS, None, ALU.add).then_inc(B[l]["var_ready"], 1)
                dve.wait_ge(B[l]["sd_ready"], n + 1)
                chain.then(v.reciprocal(rstd[:], std[:]))
                free()
                for t in range(TC):
                    last = v.tensor_scalar(xn[u][:, t], x_res[:, ds(c * TC + t, 1)].rearrange("p o d -> p (o d)"),
                                           mean_var[:, t, 0:1], rstd[:, t:t + 1], ALU.subtract, ALU.mult)
                last.then_inc(B[l]["xn_ready"], 1)

            def project(l):
                s = B[l]

                def cut(f, parts, chain, s_ready):
                    chain.then(v.tensor_copy(parts[:, 0], f))
                    chain.then(v.tensor_tensor(rest, f, parts[:, 0], ALU.subtract))
                    chain.then(v.tensor_copy(parts[:, 1], rest))
                    v.tensor_tensor(parts[:, 2], rest, parts[:, 1], ALU.subtract).then_inc(s_ready, 1)

                def step(c, u):
                    chain = Steps(dve, s["chunk_step"], c * 9)
                    normalise(l, c, u, chain, c,
                              lambda: after(dve, s["tr_mm"], c - 1))
                    dve.wait_ge(s["kf_ready"], c + 1)
                    after(dve, s["k_stored"], c * 16)
                    cut(kf, k_parts, chain, s["kparts_ready"])
                    dve.wait_ge(s["v_mm"], c + 1)
                    for t in range(TC):
                        last = v.tensor_tensor(v_all[:, ds(c * TC + t, 1), :, 0:HD].rearrange("p o h d -> p (o h) d"),
                                               vP[:, t // 2, (t % 2) * D:(t % 2 + 1) * D].rearrange("p (h d) -> p h d", h=H),
                                               bvo[:, 0].rearrange("p (h d) -> p h d", h=H), ALU.add)
                    last.then_inc(s["v_ready"], 1)
                    dve.wait_ge(s["qf_ready"], c + 1)
                    after(dve, s["q_stored"], c * 16)
                    cut(qf, q_parts, chain, s["qparts_ready"])

                dve.wait_ge(s["w_in"], 6 * 16)
                dve.wait_ge(s["ones_set"], 1)
                in_pairs(dve, NC, step)

            def attend(l):
                s = B[l]
                KW = KV[l]
                NM = 4 * KW
                HM = H // NM

                def maxima(i, u, lo, hi):
                    after(dve, s["nmt_mm"], i - 1)
                    for m in range(lo, hi):
                        dve.wait_ge(s["max_mm"], i * NM + m + 1)
                        v.tensor_reduce(neg_max[u][:, m * HM:(m + 1) * HM], mx[m % 2].rearrange("p (h k) -> p h k", h=HM),
                                        AX.X, ALU.max, negate=True).then_inc(s["max_read"], 1)

                def keep_maxima(i):
                    dve.wait_ge(s["nmt_mm"], i + 1)
                    after(dve, s["shift_in"], i * 16)
                    v.tensor_copy(neg_maxT[:], misc[0:H, 0:P]).then_inc(s["nm_ready"], 1)

                def divide(i):
                    dve.wait_ge(s["ott_mm"], i + 1)
                    sums = misc.rearrange("p (h c) -> p h c", c=32)
                    v.reciprocal(inv_den[:], sums[:, :, HD:V1]).then_inc(s["norm_step"], 1)
                    dve.wait_ge(s["norm_step"], i + 1)
                    after(dve, s["at_mm"], i)
                    v.tensor_tensor(att[:].rearrange("p (h d) -> p h d", h=H), sums[:, :, 0:HD],
                                    inv_den[:].to_broadcast([P, H, HD]), ALU.mult).then_inc(s["norm_done"], 1)

                def add(i):
                    dve.wait_ge(s["op_mm"], i + 1)
                    x = x_res[:, ds(i, 1)].rearrange("p o d -> p (o d)")
                    v.tensor_tensor(x, misc[:, 0:D], x, ALU.add).then_inc(s["x_att"], 1)

                def step(i, u):
                    first, final = isinstance(i, int) and i == 0, isinstance(i, int) and i == T - 1
                    if not final:
                        maxima(i + 1, 1 - u, 0, NM // 2)
                    if not first:
                        divide(i - 1)
                    if not final:
                        maxima(i + 1, 1 - u, NM // 2, NM)
                        keep_maxima(i + 1)
                    if not first:
                        add(i - 1)

                dve.wait_ge(s["qf_ready"], NC)
                v.memset(attP, 0.0).then_inc(s["v_ready"], 1)
                dve.wait_ge(s["bo_added"], NC)
                maxima(0, 0, 0, NM)
                keep_maxima(0)
                attend_in_pairs(dve, step)
                divide(T - 1)
                add(T - 1)

            def route(l):
                s, E = B[l], NE[l]

                def step(c, u):
                    def free():
                        dve.wait_ge(s["tr_mm"], NC + c - 1)
                        after(dve, s["xn_kept"], (c - 1) * 16)
                    chain = Steps(dve, s["chunk_step"], NC * 9 + c * 3)
                    normalise(l, c, u, chain, NC + c, free)
                    dve.wait_ge(s["r_mm"], c + 1)
                    v.tensor_tensor(logits[:, ds(c * TC, TC), 0:E], rP[u][:, 0:TC * E].rearrange("p (t e) -> p t e", t=TC),
                                    router_b[:, 0:E].rearrange("p (o e) -> p o e", o=1).to_broadcast([P, TC, E]),
                                    ALU.add).then_inc(s["lg_ready"], 1)

                dve.wait_ge(s["x_att"], T)
                in_pairs(dve, NC, step)

            def dispatch(l):
                s, E, S = B[l], NE[l], NS[l]
                chain = own[l]
                by_e = lambda x: x.rearrange("p (t o) -> p t o", o=1).to_broadcast([P, T, E])
                over_t = lambda x: x.rearrange("p (o e) -> p o e", o=1).to_broadcast([P, T, E])
                h1, h2, ha, cn, r0, r1 = (x[:, 0:T * E].rearrange("p (t e) -> p t e", t=T)
                                          for x in (hot1, hot2, hot, cnt, run0, run1))

                dve.wait_ge(s["lg_ready"], NC)
                for t in range(T):
                    last = v.max(top[:, t], logits[:, t, 0:E])
                chain.then(last)
                for t in range(T):
                    last = v.max_index(top_i[:, t], top[:, t], logits[:, t, 0:E])
                chain.then(last)
                if l == 0:
                    chain.then(v.tensor_copy(idx_f[:, 0], top_i[:, :, 0:1]))
                    v.tensor_copy(idx_f[:, 1], top_i[:, :, 1:2]).then_inc(s["routed"], 1)
                    dve.wait_ge(s["routed"], 1)
                else:
                    chain.then(v.tensor_copy(idx_f[:, 0], top_i[:, :, 0:1]))
                    chain.then(v.tensor_copy(idx_f[:, 1], top_i[:, :, 1:2]))
                    v.tensor_tensor(gap[:], top[:, :, 1], top[:, :, 0], ALU.subtract).then_inc(s["routed"], 1)
                v.tensor_tensor(h1, over_t(iota_e[:, 0:E]), idx_f[:, 0].to_broadcast([P, T, E]), ALU.is_equal)
                chain.then(v.tensor_tensor(h2, over_t(iota_e[:, 0:E]), idx_f[:, 1].to_broadcast([P, T, E]), ALU.is_equal))
                v.tensor_tensor(ha, h1, h2, ALU.add).then_inc(s["routed"], 1)

                dve.wait_ge(s["cnt_mm"], 1)
                chain.then(v.tensor_copy(cn, cntP[:, 0:T * E].rearrange("p (t e) -> p t e", t=T)))
                src, dst = cn, r0
                for d in STEPS(T):
                    v.tensor_copy(dst[:, 0:d], src[:, 0:d])
                    chain.then(v.tensor_tensor(dst[:, d:T], src[:, d:T], src[:, 0:T - d], ALU.add))
                    src, dst = dst, (r1 if dst is r0 else r0)
                run, other = src, dst
                chain.then(v.tensor_tensor(over[:, 0:E], run[:, T - 1].rearrange("p (e o) -> p e o", o=1).to_broadcast([P, E, 16]),
                                           iota_c.rearrange("p (o c) -> p o c", o=1).to_broadcast([P, E, 16]), ALU.is_gt))
                chain.then(v.reduce_sum(tiles_e[:, 0:E], over[:, 0:E], axis=AX.X))
                src, dst = tiles_e, end0
                for d in STEPS(E):
                    v.tensor_copy(dst[:, 0:d], src[:, 0:d])
                    chain.then(v.tensor_tensor(dst[:, d:E], src[:, d:E], src[:, 0:E - d], ALU.add))
                    src, dst = dst, (end1 if dst is end0 else end0)
                end = src
                chain.then(v.tensor_tensor(le[:, 0:S, 0:E], end[:, 0:E].rearrange("p (o e) -> p o e", o=1).to_broadcast([P, S, E]),
                                           iota_s[:, 0:S].rearrange("p (s o) -> p s o", o=1).to_broadcast([P, S, E]), ALU.is_le))
                chain.then(v.reduce_sum(exp_f[:, 0:S], le[:, 0:S, 0:E], axis=AX.X))
                chain.then(v.tensor_scalar(expert[:, 0:S], exp_f[:, 0:S], float(E - 1), None, ALU.min))
                chain.then(v.tensor_tensor(base[:, 0:E], end[:, 0:E], tiles_e[:, 0:E], ALU.subtract))
                chain.then(v.tensor_scalar(base[:, 0:E], base[:, 0:E], float(P), None, ALU.mult))
                chain.then(v.tensor_tensor(other, run, cn, ALU.subtract))
                chain.then(v.tensor_tensor(other, other, over_t(base[:, 0:E]), ALU.add))
                chain.then(v.tensor_tensor(other, posP[:, 0:T * E].rearrange("p (t e) -> p t e", t=T), other, ALU.add))
                for i, h in enumerate((h1, h2)):
                    chain.then(v.tensor_tensor(cn, h, other, ALU.mult))
                    chain.then(v.reduce_sum(slot_f[:, i], cn, axis=AX.X))
                v.tensor_copy(slot[:], slot_f[:]).then_inc(s["routed"], 1)

                if l == 1:
                    dve.wait_ge(s["gates_ready"], 1)
                    dve.wait_ge(s["routed"], 3)
                    chain.then(v.tensor_scalar(slot_f[:, 0], gap[:], 1.0, None, ALU.add))
                    chain.then(v.reciprocal(gates[:, :, 0], slot_f[:, 0]))
                    chain.then(v.tensor_tensor(gates[:, :, 1], gates[:, :, 0], gap[:], ALU.mult))

            def shared():
                def step(c, u):
                    for m in range(SHB):
                        dve.wait_ge(sh["u_mm"], c * SHB + m + 1)
                        dve.wait_ge(sh["act"], c * SHB + m + 1)
                        if m == 0:
                            after(dve, sh["d_mm"], c - 1)
                        v.tensor_tensor(sh_hid[u][:, m], suP[m % 2], hid[:, (m % 2) * 512:(m % 2 + 1) * 512], ALU.mult).then_inc(sh["hid"], 1)
                    dve.wait_ge(sh["d_mm"], c + 1)
                    x = x_res[:, ds(c * TC, TC)].rearrange("p (b t) d -> p b (t d)", b=2)
                    v.tensor_tensor(x, sdP, x, ALU.add).then_inc(sh["x"], 1)

                in_pairs(dve, NC, step)

            def turn_rows(s, i, u):
                dve.wait_ge(s["xt_mm"], i + 1)
                after(dve, s["up_mm"], i - 2)
                v.tensor_copy(rowsT[u].rearrange("p k t -> p (k t)"), rowsTP[:, 0:D]).then_inc(s["rowsT_ready"], 1)

            def experts0():
                s = B[0]

                def step(i, u):
                    left = NS[0] - 1 - i if isinstance(i, int) else NS[0]
                    if isinstance(i, int) and i == 0:
                        hidden(i)
                    if left > 0:
                        hidden_next(i)
                    dve.wait_ge(s["dn_mm"], i + 1)
                    if not (isinstance(i, int) and i < RING):
                        dve.wait_ge(s["y_stored"][u], (i // RING) * 16)
                    v.tensor_copy(y_rows[u], yP).then_inc(s["y_ready"], 1)
                    if left > 1:
                        turn_rows(s, i + 2, (u + 2) % RING)

                def hidden(i):
                    dve.wait_ge(s["up_mm"], i + 1)
                    dve.wait_ge(s["hid_a"], i + 1)
                    after(dve, s["ht_mm"], i)
                    v.tensor_tensor(hid[:, 0:D], upP[:, 0, D:2 * D], gate_act, ALU.mult).then_inc(s["hid_v"], 1)

                def hidden_next(i):
                    hidden(i + 1)

                turn_rows(s, 0, 0)
                turn_rows(s, 1, 1)
                in_rings(dve, NS[0], step)

            def experts1():
                s = B[1]

                def copy_hidden(i):
                    dve.wait_ge(s["up_mm"], i + 1)
                    after(dve, s["ht_mm"], 2 * i)
                    v.tensor_copy(hid[:, 512:1024], upP[:, 1]).then_inc(s["hid_v"], 1)

                def step(i, u):
                    left = NS[1] - 1 - i if isinstance(i, int) else NS[1]
                    dve.wait_ge(s["ht_mm"], 2 * i + 2)
                    dve.wait_ge(s["dn_in"][u], (i // RING + 1) * 48)
                    after(dve, s["dn_mm"], i)
                    for k in range(4, 8):
                        last = v.tensor_scalar(hidT[:, k], hidTP[:, 1, (k - 4) * P:(k - 3) * P], b1_col[u][:, k:k + 1], 0.0, ALU.add, ALU.max)
                    last.then_inc(s["hidT_v"], 1)
                    if left > 0:
                        copy_hidden(i + 1)
                    dve.wait_ge(s["dn_mm"], i + 1)
                    if not (isinstance(i, int) and i < RING):
                        dve.wait_ge(s["y_stored"][u], (i // RING) * 16)
                    v.tensor_tensor(y_rows[u], yP, b2_row[u], ALU.add).then_inc(s["y_ready"], 1)
                    if left > 1:
                        turn_rows(s, i + 2, (u + 2) % RING)

                turn_rows(s, 0, 0)
                copy_hidden(0)
                turn_rows(s, 1, 1)
                in_rings(dve, NS[1], step)

            def combine(l):
                s = B[l]
                chain = own[l]
                dve.wait_ge(s["gates_ready"], 1)
                for g in range(GROUPS):
                    dve.wait_ge(s["gathered"][g], 2 * T // GROUPS * 16)
                    for i in range(2):
                        for t in range(g * T // GROUPS, (g + 1) * T // GROUPS):
                            last = v.scalar_tensor_tensor(out=x_res[:, t], in0=y_got[:, t, i], scalar=gates[:, t, i:i + 1],
                                                          in1=x_res[:, t], op0=ALU.mult, op1=ALU.add)
                            if i == 1:
                                last.then_inc(s["x_ffn"], 1)
                        if i == 0:
                            chain.then(last)

            dve.wait_ge(once["x_in"], 16)
            dve.wait_ge(once["consts_in"], 16)
            for l in range(2):
                if l:
                    dve.wait_ge(B[0]["x_ffn"], T)
                project(l)
                attend(l)
                route(l)
                dispatch(l)
                if l == 0:
                    shared()
                    experts0()
                else:
                    experts1()
                combine(l)

        @block.gpsimd
        def _(pool):
            pool.memset(zeros, 0.0).then_inc(once["zeros_set"], 1)
            for l in range(2):
                s = B[l]
                if l:
                    pool.wait_ge(B[0]["x_ffn"], T)
                pool.wait_ge(once["zeros_set"], 1)
                pool.memset(v_all, 1.0).then_inc(s["ones_set"], 1)
                pool.wait_ge(s["ones_set"], 1)
                pool.memset(k_stack[KR:KR + 1], 1.0).then_inc(s["ones_set"], 1)
                pool.wait_ge(s["ones_set"], 2)
                pool.wait_ge(s["w_in"], 6 * 16)

                def add_bias(c, u):
                    pool.wait_ge(s["xn_ready"], c + 1)
                    x = x_res[:, ds(c * TC, TC)]
                    pool.tensor_tensor(x, x, bvo[:, 1:2].to_broadcast([P, TC, D]), ALU.add).then_inc(s["bo_added"], 1)

                in_pairs(pool, NC, add_bias)

                pool.wait_ge(once["slots_zeroed"], 16)
                pool.wait_ge(s["xn_kept"], NC * 16)
                pool.wait_ge(s["routed"], 3)
                for t in range(T):
                    for i in range(2):
                        pool.indirect_dma_start(slot_in, bass.IndirectOffsetOnAxis(ap=slot[:, i, t:t + 1], axis=0),
                                                xn_all[:, t], None).then_inc(s["scattered"], 16)
                for u in range(RING):
                    pool.wait_ge(s["y_stored"][u], NS[l] // RING * 16)
                for g in range(GROUPS):
                    for t in range(g * T // GROUPS, (g + 1) * T // GROUPS):
                        for i in range(2):
                            pool.indirect_dma_start(y_got[:, t, i], None, slot_out[l],
                                                    bass.IndirectOffsetOnAxis(ap=slot[:, i, t:t + 1], axis=0)).then_inc(s["gathered"][g], 16)


def kernel(**inputs):
    import numpy as np
    import concourse.bacc as bacc
    from concourse import mybir as mb
    from concourse.bass_utils import run_bass_kernel_spmd as run

    g = {k: np.asarray(v) for k, v in inputs.items()}
    shape = g["x"].shape
    d = shape[-1]
    p = 128
    c = np.zeros((p, 3 * p + 32 + 48), np.float32)
    c[:, 0:p] = np.eye(p)
    c[:, p:2 * p] = np.arange(p)[:, None] < np.arange(p)[None, :]
    c[:, 2 * p:3 * p] = 1
    c[:, 3 * p:3 * p + 16] = np.arange(16)
    c[:, 3 * p + 16:3 * p + 32] = p * np.arange(16)
    c[:, 3 * p + 32:] = np.arange(48)
    cols = lambda b: b.reshape(2, p).T
    w0, b0 = g["L0_xattn_in_proj_w"], g["L0_xattn_in_proj_b"]
    arrays = {
        "x": g["x"].reshape(-1, d), "ctxT": g["ctx_1024"].reshape(-1, d).T, "consts": c,
        "att_w0": np.concatenate([w0[0:d].T, w0[d:2 * d].T, w0[2 * d:].T, g["L0_xattn_out_w"].T]),
        "att_w1": np.concatenate([g[f"L1_xattn_W{n}"].T for n in "qkvo"]),
        "bqk0": np.concatenate([cols(b0[0:d]), cols(b0[d:2 * d])], 1),
        "bqk1": np.concatenate([cols(g["L1_xattn_bq"]), cols(g["L1_xattn_bk"])], 1),
        "bvo0": np.stack([b0[2 * d:], g["L0_xattn_out_b"]]), "bvo1": np.stack([g["L1_xattn_bv"], g["L1_xattn_bo"]]),
        "router_w0": g["L0_ffn_router_w"].T, "router_w1": g["L1_ffn_W_router"],
        "router_b0": np.zeros((1, 16), np.float32), "router_b1": g["L1_ffn_b_router"][None],
        "sh_gate": g["L0_ffn_shared_gate_w"].T, "sh_up": g["L0_ffn_shared_up_w"].T, "sh_down": g["L0_ffn_shared_down_w"].T,
        "exp_up0": g["L0_ffn_gate_up_w"], "exp_dn0": g["L0_ffn_down_w"],
        "exp_up1": g["L1_ffn_W1"], "exp_dn1": g["L1_ffn_W2"],
        "exp_b1": g["L1_ffn_b1"].reshape(8, 8, p).transpose(0, 2, 1), "exp_b2": g["L1_ffn_b2"],
    }
    arrays = {k: np.ascontiguousarray(v) for k, v in arrays.items()}
    nc = bacc.Bacc("TRN2", target_bir_lowering=False, num_devices=1)
    aps = {k: nc.dram_tensor(f"in_{k}", v.shape, mb.dt.from_np(v.dtype), kind="ExternalInput").ap() for k, v in arrays.items()}
    out = nc.dram_tensor("out", (shape[0] * shape[1], d), mb.dt.float32, kind="ExternalOutput").ap()
    xattn_moe_program(nc, aps, out)
    got = run(nc, [{f"in_{k}": v for k, v in arrays.items()}], core_ids=[0]).results[0]["out"]
    return got.reshape(shape)
```

```python
from contextlib import ExitStack

import concourse.bass as bass
from concourse import mybir


def xattn_moe_program(nc, a, out):
    F32, BF16, F16 = mybir.dt.float32, mybir.dt.bfloat16, mybir.dt.float16
    U32, I32 = mybir.dt.uint32, mybir.dt.int32
    ALU, ACT, AX = mybir.AluOpType, mybir.ActivationFunctionType, mybir.AxisListType
    ds = bass.ds

    P = 128
    N, D = a["x"].shape
    T = N // P
    KD = D // P
    TC = 4
    CW = TC * P
    NC = T // TC
    H, HD = 16, 16
    HB = P // HD
    PARTS = 3
    QK = [(0, 0), (0, 1), (1, 0), (1, 1), (0, 2), (2, 0)]
    KR = len(QK) * HD
    SCALE = float(HD) ** -0.5
    EPS = 1e-5
    V1 = HD + 1
    KV = [1, 2]
    NE = [16, 8]
    NS = [48, 39]
    QUAD = 4
    SPREAD = [[0, 1, 3, 4, 4], [0, 2, 3, 4, 5, 7, 8]]
    GROUPS = NC
    SH = 512
    SHB = SH // P
    UPW = [512, 1024]
    HK = [2, 8]
    WCOL = [KD * UPW[l] + HK[l] * D for l in range(2)]
    PIECES = 16
    PER = [PIECES // e for e in NE]
    PCOL = [WCOL[l] // PER[l] for l in range(2)]
    AHEAD = 5
    WS = 64.0
    HS = [64.0, 1.0]
    PASSES = [(0, 0), (1, 0), (0, 1)]
    assert all(s * P >= 2 * N + (e - 1) * (P - 1) for s, e in zip(NS, NE)) and NS[0] % T == 0
    STEPS = lambda n: [1 << i for i in range((n - 1).bit_length())]

    ctx = ExitStack()
    with ctx:
        def sb(name, shape, dt=F32):
            return ctx.enter_context(nc.sbuf_tensor(name, shape, dt))

        def sem(name):
            return ctx.enter_context(nc.semaphore(name))

        def dram(name, shape, dt):
            return nc.dram_tensor(name, shape, dt, kind="Internal").ap()

        q_parts_d = [dram(f"q_parts_d{l}", (NC, P, PARTS, KD, CW), BF16) for l in range(2)]
        k_parts_d = [dram(f"k_parts_d{l}", (NC, P, PARTS, KD, CW), BF16) for l in range(2)]
        slot_in = dram("slot_in", (NS[0] * P, D), F32)
        slot_out = [dram(f"slot_out{l}", (NS[l] * P, D), F32) for l in range(2)]

        x_res = sb("x_res", [P, T, D])
        consts = sb("consts", list(a["consts"].shape))
        ident, ltri, ones = consts[:, 0:P], consts[:, P:2 * P], consts[:, 2 * P:3 * P]
        iota_e = consts[:, 3 * P:3 * P + 16]
        iota_c = consts[:, 3 * P + 16:3 * P + 32]
        iota_s = consts[:, 3 * P + 32:3 * P + 32 + 48]

        arena = sb("arena", [P, 38656])
        k_stack = arena[:, 0:16384].bitcast(BF16).rearrange("p (h t) -> p h t", h=H)
        q_stack = arena[:, 16384:24576].bitcast(BF16).rearrange("p (h t) -> p h t", h=H)
        arena2, arena3, arena4 = arena[:, 24576:28672], arena[:, 28672:33024], arena[:, 33024:38656]
        wts_flat = arena[:, :].bitcast(F16)
        wts = [arena[:, 0:PIECES * PCOL[l]].bitcast(F16).rearrange("p (q c) -> p q c", c=PCOL[l]) for l in range(2)]
        keep_at = [20480, 28672]
        xn_all = [arena[:, w:w + T * D].rearrange("p (t d) -> p t d", t=T) for w in keep_at]
        FREE = [keep_at[l] // PCOL[l] for l in range(2)]
        y_got = arena[:, 16384:16384 + 2 * T * D].rearrange("p (t s d) -> p t s d", t=T, s=2)

        qf = arena2[:, 0:1024].rearrange("p (m t) -> p m t", m=KD)
        kf = arena2[:, 1024:2048].rearrange("p (m t) -> p m t", m=KD)
        rest = arena2[:, 2048:3072].rearrange("p (m t) -> p m t", m=KD)
        probs = [arena2[:, 1024 * i:1024 * (i + 1)] for i in range(4)]
        sh_hid = [arena2[:, 2048 * u:2048 * (u + 1)].rearrange("p (m t) -> p m t", m=SHB) for u in range(2)]

        v_all = arena3[:, 0:T * H * V1].rearrange("p (t h c) -> p t h c", t=T, h=H)
        xnT_all = arena3[:, 0:KD * N].rearrange("p (k t) -> p k t", k=KD)

        ctxT = [arena4[:, 1024 * u:1024 * (u + 1)].rearrange("p (k t) -> p k t", k=KD) for u in range(2)]
        q_parts = arena4[:, 2048:3584].bitcast(BF16).rearrange("p (s m t) -> p s m t", s=PARTS, m=KD)
        k_parts = arena4[:, 3584:5120].bitcast(BF16).rearrange("p (s m t) -> p s m t", s=PARTS, m=KD)
        rows = [arena4[:, 256 * u:256 * (u + 1)] for u in range(2)]
        rowsT = [[arena4[:, 512 + 128 * (2 * u + part):640 + 128 * (2 * u + part)].bitcast(F16).rearrange("p (k t) -> p k t", k=KD)
                  for part in range(2)] for u in range(2)]
        hid = arena4[:, 1536:2560]
        gate_act = [arena4[:, 2048 + 256 * u:2304 + 256 * u] for u in range(2)]
        hidT = [[arena4[:, 2560 + 512 * (2 * u + part):3072 + 512 * (2 * u + part)].bitcast(F16).rearrange("p (k t) -> p k t", k=8)
                 for part in range(2)] for u in range(2)]
        y_rows = [arena4[:, 4608 + 256 * u:4864 + 256 * u] for u in range(2)]
        b2_row = [arena4[:, 5120 + 256 * u:5376 + 256 * u] for u in range(2)]
        b1_col = [arena4[:, 1024 + 8 * u:1032 + 8 * u] for u in range(2)]
        zeros = arena4[:, 5120:5376]

        xn_buf, xnT_buf = sb("xn_buf", [P, 2048]), sb("xnT_buf", [P, 2048])
        xn = [xn_buf[:, 1024 * u:1024 * (u + 1)].rearrange("p (t d) -> p t d", t=TC) for u in range(2)]
        xnT = [xnT_buf[:, 1024 * u:1024 * (u + 1)].rearrange("p (k t) -> p k t", k=KD) for u in range(2)]
        sh_gate, sh_up = (xn_buf[:, 1024 * u:1024 * (u + 1)].rearrange("p (k n) -> p k n", k=KD) for u in range(2))
        sh_down = xnT_buf[:, 0:1024].rearrange("p (k n) -> p k n", k=SHB)
        place = lambda l, q: arena[:, q * PCOL[l]:(q + 1) * PCOL[l]]
        staged0 = [(arena4[:, 0:1536], place(0, 12) if q < 8 else arena4[:, 2560:4096], place(0, 11) if q < 9 else arena4[:, 4096:5632])[q % 3]
                   for q in range(PIECES)]
        staged1 = [place(1, FREE[1] - 1 - q % AHEAD) if q < AHEAD + 3 else (xn_buf, xnT_buf, arena4)[(q - AHEAD - 3) % 3][:, 0:PCOL[1]] for q in range(PIECES)]
        staged = [staged0, staged1]
        stager = [q - AHEAD if AHEAD <= q < AHEAD + 3 else q - 3 if q >= AHEAD + 6 else -1 for q in range(PIECES)]
        att_w = sb("att_w", [P, 4, KD, D])
        wq, wk, wv, wo = (att_w[:, i] for i in range(4))
        bqk = sb("bqk", [P, 2, KD])
        bvo = sb("bvo", [P, 2, D])
        router_w = sb("router_w", [P, KD, 16])
        router_b = sb("router_b", [P, 16])
        v_tile = [sb(f"v_tile{u}", [P, 2, H, V1]) for u in range(2)]
        stats = sb("stats", [P, TC, 6])
        mean_var = sb("mean_var", [P, TC, 2])
        var_eps, std, rstd = (sb(n, [P, TC]) for n in ("var_eps", "std", "rstd"))
        neg_max = [sb(f"neg_max{u}", [P, H]) for u in range(2)]
        neg_maxT = sb("neg_maxT", [H, P], BF16)
        att_raw = sb("att_raw", [P, 512])
        inv_den = sb("inv_den", [P, H, 1])
        att = sb("att", [P, D])
        attT = sb("attT", [P, KD, P])
        logits = sb("logits", [P, T, 16])
        top = sb("top", [P, T, 8])
        top_i = sb("top_i", [P, T, 8], U32)
        idx_f = sb("idx_f", [P, 2, T, 1])
        hot1, hot2, hot, cnt, run0, run1 = (arena4[:, 2560 + 256 * i:2560 + 256 * (i + 1)] for i in range(6))
        over = arena4[:, 4096:4352].rearrange("p (e c) -> p e c", c=16)
        tiles_e, end0, end1, base = (sb(n, [P, 16]) for n in ("tiles_e", "end0", "end1", "base"))
        slot_f = sb("slot_f", [P, 2, T])
        slot = sb("slot", [P, 2, T], I32)
        le = arena4[:, 4352:5120].rearrange("p (s e) -> p s e", e=16)
        exp_f = sb("exp_f", [P, 48])
        expert = sb("expert", [P, 48], I32)
        packed_f = sb("packed_f", [P, 48])
        packed = sb("packed", [P, 48], I32)
        gates = sb("gates", [P, T, 2])
        gap = sb("gap", [P, T])

        bank = ctx.enter_context(nc.psum_tensor("bank", [P, 8, 512], F32))
        trT = bank[:, 0:2]
        kP, vP, qP = bank[:, 2:4], bank[:, 4:6], bank[:, 6:8]
        mx = [bank[:, 0], bank[:, 1]]
        sc = [bank[:, 2:4], bank[:, 4:6]]
        attP, misc = bank[:, 6], bank[:, 7]
        rP = [bank[:, 2], bank[:, 3]]
        posP, cntP = bank[:, 4], bank[:, 5]
        sgP, suP = [bank[:, 0], bank[:, 1]], [bank[:, 2], bank[:, 3]]
        sdP = bank[:, 6:8]
        upP = [bank[:, 2 * u:2 * u + 2] for u in range(2)]
        yP = [bank[:, 4 + u, 0:D] for u in range(2)]
        rowsTP = [bank[:, 6 + u, 0:D] for u in range(2)]

        once = {n: sem(n) for n in ("inputs_in", "zeros_set", "slots_zeroed", "out_stored")}

        def block_sems(l):
            names = """w_in var_ready sd_ready xn_ready bo_added k_mm v_mm tr_mm q_mm kf_ready xT_ready qf_ready
                kparts_ready qparts_ready v_ready ones_set k_stored q_stored k_in q_in chunk_step
                max_mm max_read nmt_mm nm_ready shift_in sc_mm exp_done pv_mm raw_ready ott_mm norm_step
                norm_done at_mm atT_ready op_mm x_att
                r_mm lg_ready xn_kept
                step routed cnt_mm gates_ready scattered
                w_hi w_lo xt_mm rows_hi rowsT_ready up_mm hid_a hidT_ready dn_mm y_ready x_ffn""".split()
            s = {n: sem(f"{n}_{l}") for n in names}
            s["ctx_in"] = [sem(f"ctx_in{u}_{l}") for u in range(2)]
            s["v_in"] = [sem(f"v_in{u}_{l}") for u in range(2)]
            if l == 0:
                s["hid_v"] = sem("hid_v_0")
            s["w_staged"] = [sem(f"w_staged{u}_{l}") for u in range(AHEAD + 1 if l else 3)]
            for n in ("rows_in", "y_stored") + (("b1_in", "b2_in") if l else ()):
                s[n] = [sem(f"{n}{u}_{l}") for u in range(2)]
            s["gathered"] = [sem(f"gathered{g}_{l}") for g in range(2)]
            return s

        B = [block_sems(l) for l in range(2)]
        sh = {n: sem(f"sh_{n}") for n in ("w_in", "xT_kept", "gu_mm", "act", "hid", "d_mm", "x")}

        class Steps:
            def __init__(self, eng, s, start=0):
                self.eng, self.sem, self.start, self.n = eng, s, start, 0

            def then(self, ins):
                self.n += 1
                ins.then_inc(self.sem, 1)
                self.eng.wait_ge(self.sem, self.start + self.n)

        def after(eng, s, count):
            if not (isinstance(count, int) and count <= 0):
                eng.wait_ge(s, count)

        def in_pairs(eng, n, step):
            step(0, 0)
            step(1, 1)
            with eng.Fori(1, n // 2) as j:
                for u in range(2):
                    step(j * 2 + u, u)

        def in_chunks(step):
            for c in range(NC):
                step(c, c % 2)

        def in_all_pairs(eng, n, step):
            step(0, 0)
            step(1, 1)
            with eng.Fori(1, n // 2 - 1) as j:
                for u in range(2):
                    step(j * 2 + u, u)
            for i in range(n // 2 * 2 - 2, n):
                step(i, i % 2)

        def least(x, top):
            return min(x, top) if isinstance(x, int) else x

        block = ctx.enter_context(nc.Block())

        @block.sync
        def _(sp):
            def load_attention_weights(l):
                s = B[l]
                if l:
                    sp.wait_ge(B[0]["x_att"], T)
                    sp.wait_ge(B[0]["lg_ready"], NC)
                sp.dma_start(att_w[:].rearrange("p w k n -> p (w k) n"),
                             a[f"att_w{l}"].rearrange("(q p) n -> p q n", p=P)).then_inc(s["w_in"], 16)
                sp.dma_start(bqk[:].rearrange("p b m -> p (b m)"), a[f"bqk{l}"]).then_inc(s["w_in"], 16)
                for i in range(2):
                    sp.dma_start(bvo[:, i], a[f"bvo{l}"][i:i + 1, :].to_broadcast([P, D])).then_inc(s["w_in"], 16)
                sp.dma_start(router_w[:, :, 0:NE[l]],
                             a[f"router_w{l}"].rearrange("(k p) e -> p k e", p=P)).then_inc(s["w_in"], 16)
                sp.dma_start(router_b[:, 0:NE[l]], a[f"router_b{l}"].to_broadcast([P, NE[l]])).then_inc(s["w_in"], 16)

            def store_parts(parts_d, c, parts, s_stored):
                sp.dma_start(parts_d[ds(c, 1)].rearrange("o p s m t -> p (o s m t)"),
                             parts.rearrange("p s m t -> p (s m t)")).then_inc(s_stored, 16)

            def stack(dst, parts_d, c, which, column, s_in):
                src = parts_d[ds(c, 1)].rearrange("o (h r) s m t -> r (o s m) h t", r=HD)
                for b, pair in enumerate(QK):
                    for m in range(KD):
                        sp.dma_start(dst[HD * b:HD * (b + 1), HB * m:HB * (m + 1), ds(column, CW)],
                                     src[:, pair[which] * KD + m]).then_inc(s_in, 16)

            def load_queries(l, c):
                s = B[l]
                if not (isinstance(c, int) and c < 2):
                    sp.wait_ge(s["sc_mm"], (c - 1) * TC * 2 * KV[l])
                after(sp, s["q_in"], c * len(QK) * KD * 16)
                sp.wait_ge(s["q_stored"], c * 16 + 16)
                stack(q_stack, q_parts_d[l], c, 0, (c % 2) * CW, s["q_in"])

            def project(l):
                s = B[l]

                def load_context(c, u):
                    after(sp, s["v_mm"], c - 1)
                    sp.dma_start(ctxT[u], a["ctxT"].rearrange("(k p) t -> p k t", p=P)[:, :, ds(c * CW, CW)]).then_inc(s["ctx_in"][u], 16)

                def step(c, u):
                    if c + 1 < NC:
                        load_context(c + 1, 1 - u)
                    else:
                        if l:
                            sp.wait_ge(B[0]["x_ffn"], T)
                        load_queries(l, 0)
                    sp.wait_ge(s["kparts_ready"], c + 1)
                    store_parts(k_parts_d[l], c, k_parts, s["k_stored"])
                    sp.wait_ge(s["k_stored"], c * 16 + 16)
                    sp.wait_ge(s["k_in"], (c * len(QK) * KD + 1) * 16)
                    stack(k_stack, k_parts_d[l], c, 1, c * CW, s["k_in"])
                    sp.wait_ge(s["qparts_ready"], c + 1)
                    store_parts(q_parts_d[l], c, q_parts, s["q_stored"])

                load_context(0, 0)
                sp.dma_start(k_stack[KR:KR + 1].rearrange("o h t -> o (h t)"), a["ones_row"].bitcast(BF16)).then_inc(s["k_in"], 16)
                in_chunks(step)

            def attend(l):
                s = B[l]
                KW = KV[l]

                def load_values(i, u):
                    after(sp, s["pv_mm"], 2 * (i - 1))
                    first = i if KW == 1 else (i // 2) * 2
                    sp.dma_start(v_tile[u][:, 0:KW].rearrange("p k h c -> p (k h c)"),
                                 v_all[:, ds(first, KW)].rearrange("p k h c -> p (k h c)")).then_inc(s["v_in"][u], 16)

                def place_shift(i):
                    sp.wait_ge(s["nm_ready"], i + 1)
                    sp.dma_start(q_stack[KR:KR + 1, :, ds((i % (2 * TC)) * P, P)], neg_maxT[:]).then_inc(s["shift_in"], 16)

                sp.wait_ge(s["v_ready"], NC)
                load_values(0, 0)
                place_shift(0)
                load_queries(l, 1)
                if l == 0:
                    sp.wait_ge(once["zeros_set"], 1)

                def clear_slots(i):
                    n = NS[0] // T
                    sp.dma_start(slot_in[ds(i * n * P, n * P), :].rearrange("(p r) d -> p r d", p=P),
                                 zeros.rearrange("p (o w) -> p o w", o=1).to_broadcast([P, n, D])).then_inc(once["slots_zeroed"], 16)

                def chunk(c, more):
                    for t in range(TC):
                        if l == 0:
                            clear_slots(c * TC + t)
                        if more or t < TC - 1:
                            load_values(c * TC + t + 1, (t + 1) % 2)
                            place_shift(c * TC + t + 1)
                    if more is True:
                        load_queries(l, c + 2)

                with sp.Fori(0, NC - 2) as c:
                    chunk(c, True)
                chunk(NC - 2, 1)
                chunk(NC - 1, 0)

            def route(l):
                s = B[l]
                sp.wait_ge(s["x_att"], T)
                if l:
                    load_weights1(0, AHEAD)

                def step(c, u):
                    sp.wait_ge(s["xn_ready"], NC + c + 1)
                    sp.dma_start(xn_all[l][:, ds(c * TC, TC)].rearrange("p t d -> p (t d)"),
                                 xn[u].rearrange("p t d -> p (t d)")).then_inc(s["xn_kept"], 16)
                    if l == 0:
                        sp.wait_ge(s["xT_ready"], NC + c + 1)
                        sp.dma_start(xnT_all[:, :, ds(c * CW, CW)], xnT[u]).then_inc(sh["xT_kept"], 16)
                        if c == NC - 1:
                            sp.wait_ge(s["tr_mm"], 2 * NC)
                            sp.dma_start(sh_gate, a["sh_gate"].rearrange("(k p) n -> p k n", p=P)).then_inc(sh["w_in"], 16)
                            sp.wait_ge(s["r_mm"], c)
                            sp.dma_start(sh_down, a["sh_down"].rearrange("(k p) n -> p k n", p=P)).then_inc(sh["w_in"], 16)
                        sp.wait_ge(sh["xT_kept"], c * 16 + 16)
                    sp.wait_ge(s["xn_kept"], c * 16 + 16)
                    if l == 0 and c == NC - 1:
                        sp.dma_start(sh_up, a["sh_up"].rearrange("(k p) n -> p k n", p=P)).then_inc(sh["w_in"], 16)

                in_chunks(step)

            def load_weights0():
                s, up, dn, first = B[0], a["exp_up0"], a["exp_dn0"], KD * UPW[0]
                for q in range(PIECES):
                    if q == 9:
                        sp.wait_ge(s["routed"], 3)
                    if q >= 3:
                        sp.wait_ge(s["w_lo"], q - 2)
                    sp.dma_start(staged[0][q][:, 0:first].rearrange("p (k n) -> p k n", k=KD),
                                 up[q].rearrange("(k p) n -> p k n", p=P)).then_inc(s["w_staged"][q % 3], 16)
                    sp.dma_start(staged[0][q][:, first:WCOL[0]].rearrange("p (k n) -> p k n", k=HK[0]),
                                 dn[q].rearrange("(k p) n -> p k n", p=P)).then_inc(s["w_staged"][q % 3], 16)

            def load_weights1(lo, hi):
                s = B[1]
                for q in range(lo, hi):
                    if q == AHEAD + 3:
                        sp.wait_ge(s["tr_mm"], 2 * NC)
                        sp.wait_ge(s["r_mm"], NC)
                    if q > AHEAD or stager[q] >= 0:
                        sp.wait_ge(s["w_lo"], max(stager[q], q - AHEAD - 1) + 1)
                    w, k = (a["exp_up1"], KD) if q % 2 == 0 else (a["exp_dn1"], HK[1])
                    sp.dma_start(staged[1][q].rearrange("p (k n) -> p k n", k=k),
                                 w[q // 2].rearrange("(k p) n -> p k n", p=P)).then_inc(s["w_staged"][q % (AHEAD + 1)], 16)

            def experts(l):
                s, S = B[l], NS[l]
                sp.wait_ge(s["routed"], 3)
                sp.wait_ge(s["w_lo"], PIECES)

                def step(i, u):
                    if l == 1:
                        e = sp.value_load(expert[0:1, ds(i, 1)], min_val=0, max_val=NE[l] - 1)
                        after(sp, s["hid_a"], (i - 1) * 2)
                        sp.dma_start(b1_col[u], a["exp_b1"][ds(e, 1)].rearrange("o p k -> p (o k)")).then_inc(s["b1_in"][u], 16)
                    if not (isinstance(i, int) and i < 2):
                        store_rows(i - 2, u)
                    if l == 1:
                        sp.dma_start(b2_row[u], a["exp_b2"][ds(e, 1)].to_broadcast([P, D])).then_inc(s["b2_in"][u], 16)

                def store_rows(i, u):
                    sp.wait_ge(s["y_ready"], i + 1)
                    sp.dma_start(slot_out[l][ds(i * P, P), :], y_rows[u]).then_inc(s["y_stored"][u], 16)

                in_all_pairs(sp, S, step)
                for i in range(S - 2, S):
                    store_rows(i, i % 2)

            sp.dma_start(x_res[:], a["x"].rearrange("(t p) d -> p t d", p=P)).then_inc(once["inputs_in"], 16)
            sp.dma_start(consts[:], a["consts"]).then_inc(once["inputs_in"], 16)
            for l in range(2):
                load_attention_weights(l)
                if l:
                    for u in range(2):
                        sp.wait_ge(B[0]["y_stored"][u], NS[0] // 2 * 16)
                project(l)
                attend(l)
                route(l)
                if l == 0:
                    load_weights0()
                else:
                    load_weights1(AHEAD, PIECES)
                experts(l)
            for g in range(GROUPS):
                sp.wait_ge(B[1]["x_ffn"], (g + 1) * T // GROUPS)
                of_group = slice(g * T // GROUPS, (g + 1) * T // GROUPS)
                sp.dma_start(out.rearrange("(t p) d -> p t d", p=P)[:, of_group], x_res[:, of_group]).then_inc(once["out_stored"], 16)
            sp.wait_ge(once["out_stored"], GROUPS * 16)

        @block.tensor
        def _(pe):
            mm, tr = nc.tensor.matmul, nc.tensor.transpose

            def project(l):
                s = B[l]
                pe.wait_ge(s["w_in"], 6 * 16)
                if l:
                    pe.wait_ge(B[0]["y_ready"], NS[0])

                def step(c, u):
                    pe.wait_ge(s["ctx_in"][u], (c // 2 + 1) * 16)
                    after(pe, s["kf_ready"], c)
                    for m in range(KD):
                        for k in range(KD):
                            last = mm(kP[:, m], wk[:, k, m * P:(m + 1) * P], ctxT[u][:, k], start=k == 0, stop=k == KD - 1)
                    last.then_inc(s["k_mm"], 1)
                    pe.wait_ge(s["xn_ready"], c + 1)
                    after(pe, s["xT_ready"], c)
                    for t in range(TC):
                        for k in range(KD):
                            last = tr(trT[:, k, t * P:(t + 1) * P], xn[u][:, t, k * P:(k + 1) * P], ident)
                    last.then_inc(s["tr_mm"], 1)
                    after(pe, s["v_ready"], c)
                    for t in range(TC):
                        for k in range(KD):
                            last = mm(vP[:, t // 2, (t % 2) * D:(t % 2 + 1) * D], ctxT[u][:, k, t * P:(t + 1) * P], wv[:, k],
                                      start=k == 0, stop=k == KD - 1)
                    last.then_inc(s["v_mm"], 1)
                    pe.wait_ge(s["xT_ready"], c + 1)
                    after(pe, s["qf_ready"], c)
                    for m in range(KD):
                        for k in range(KD):
                            last = mm(qP[:, m], wq[:, k, m * P:(m + 1) * P], xnT[u][:, k], start=k == 0, stop=k == KD - 1)
                    last.then_inc(s["q_mm"], 1)

                in_chunks(step)

            def attend(l):
                s = B[l]
                KW = KV[l]
                NM = 4 * KW
                HM = H // NM
                NP = 2 * KW
                keys = lambda i: i * P if KW == 1 else (i // 2) * (2 * P)

                def maxima(i, lo, hi):
                    if lo == 0:
                        pe.wait_ge(s["k_in"], ((i // TC + 1) * len(QK) * KD + 1) * 16)
                        pe.wait_ge(s["q_in"], (i // TC + 1) * len(QK) * KD * 16)
                    for m in range(lo, hi):
                        after(pe, s["max_read"], i * NM + m - 1)
                        for hh in range(HM):
                            h = m * HM + hh
                            last = mm(mx[m % 2][:, hh * KW * P:(hh + 1) * KW * P], q_stack[0:KR, h, ds((i % (2 * TC)) * P, P)],
                                      k_stack[0:KR, h, ds(keys(i), KW * P)], start=True, stop=True)
                        last.then_inc(s["max_mm"], 1)

                def turn_maxima(i, u):
                    pe.wait_ge(s["max_read"], (i + 1) * NM)
                    after(pe, s["x_att"], i - 2)
                    tr(misc[0:H, 0:P], neg_max[u][:], ident).then_inc(s["nmt_mm"], 1)

                def scores(i, p):
                    half, kv = p // KW, p % KW
                    if p == 0:
                        pe.wait_ge(s["shift_in"], (i + 1) * 16)
                    after(pe, s["exp_done"], i * NP + p - 1)
                    for hh in range(8):
                        h = half * 8 + hh
                        last = mm(sc[p % 2][:, hh // 4, (hh % 4) * P:(hh % 4 + 1) * P], k_stack[0:KR + 1, h, ds(keys(i) + kv * P, P)],
                                  q_stack[0:KR + 1, h, ds((i % (2 * TC)) * P, P)], start=True, stop=True)
                    last.then_inc(s["sc_mm"], 1)

                def values(i, u, half):
                    if half == 0:
                        pe.wait_ge(s["v_in"][u], (i // 2 + 1) * 16)
                        after(pe, s["raw_ready"], i)
                    pe.wait_ge(s["exp_done"], i * NP + (half + 1) * KW)
                    for hh in range(8):
                        h = half * 8 + hh
                        j, g = h % 4, h // 4
                        for kv in range(KW):
                            pr = probs[2 * u + half] if KW == 1 else probs[half * KW + kv]
                            last = mm(attP[32 * j:32 * j + V1, g * P:(g + 1) * P], v_tile[u][:, kv, h], pr[:, hh * P:(hh + 1) * P],
                                      start=kv == 0, stop=kv == KW - 1)
                    last.then_inc(s["pv_mm"], 1)

                def turn_back(i):
                    pe.wait_ge(s["raw_ready"], i + 1)
                    after(pe, s["x_att"], i)
                    pe.wait_ge(s["nm_ready"], least(i + 3, T))
                    for g in range(4):
                        last = tr(misc[:, g * P:(g + 1) * P], att_raw[:, g * P:(g + 1) * P], ident)
                    last.then_inc(s["ott_mm"], 1)

                def turn_attention(i):
                    pe.wait_ge(s["norm_done"], i + 1)
                    for k in range(KD):
                        last = tr(misc[:, k * P:(k + 1) * P], att[:, k * P:(k + 1) * P], ident)
                    last.then_inc(s["at_mm"], 1)

                def project_out(i):
                    pe.wait_ge(s["atT_ready"], i + 1)
                    for k in range(KD):
                        last = mm(misc[:, 0:D], attT[:, k], wo[:, k], start=k == 0, stop=k == KD - 1)
                    last.then_inc(s["op_mm"], 1)

                def step(i, u):
                    first, left = isinstance(i, int) and i == 0, T - 1 - i if isinstance(i, int) else T
                    if left > 0:
                        turn_maxima(i + 1, 1 - u)
                    for p in range(NP):
                        scores(i, p)
                        if left > 1:
                            maxima(i + 2, SPREAD[l][p], SPREAD[l][p + 1])
                        if p == 0 and not first:
                            turn_back(i - 1)
                        if p == max(NP - 2, 1) and not first:
                            turn_attention(i - 1)
                    values(i, u, 0)
                    if left > 1:
                        maxima(i + 2, SPREAD[l][NP], SPREAD[l][NP + 1])
                    if not first:
                        project_out(i - 1)
                    if left > 1:
                        maxima(i + 2, SPREAD[l][NP + 1], NM)
                    values(i, u, 1)

                pe.wait_ge(s["xT_ready"], NC)
                pe.wait_ge(s["kf_ready"], NC)
                pe.wait_ge(s["v_ready"], NC)
                pe.wait_ge(s["qf_ready"], NC)
                pe.wait_ge(s["v_ready"], NC + 1)
                maxima(0, 0, NM)
                turn_maxima(0, 0)
                maxima(1, 0, NM)
                for i in range(T):
                    step(i, i % 2)
                turn_back(T - 1)
                turn_attention(T - 1)
                project_out(T - 1)

            def route(l):
                s, E = B[l], NE[l]

                def turn_tokens(c, u):
                    pe.wait_ge(s["xn_ready"], NC + c + 1)
                    pe.wait_ge(s["xT_ready"], NC + c)
                    for t in range(TC):
                        for k in range(KD):
                            last = tr(trT[:, k, t * P:(t + 1) * P], xn[u][:, t, k * P:(k + 1) * P], ident)
                    last.then_inc(s["tr_mm"], 1)

                def step(c, u):
                    if c + 1 < NC:
                        turn_tokens(c + 1, 1 - u)
                    pe.wait_ge(s["xT_ready"], NC + c + 1)
                    after(pe, s["lg_ready"], c - 1)
                    for t in range(TC):
                        for k in range(KD):
                            last = mm(rP[u][:, t * E:(t + 1) * E], xnT[u][:, k, t * P:(t + 1) * P], router_w[:, k, 0:E],
                                      start=k == 0, stop=k == KD - 1)
                    last.then_inc(s["r_mm"], 1)

                turn_tokens(0, 0)
                in_chunks(step)

            def dispatch(l):
                s, E = B[l], NE[l]
                pe.wait_ge(s["routed"], 2)
                mm(posP[:, 0:T * E], ltri, hot[:, 0:T * E], start=True, stop=True)
                mm(cntP[:, 0:T * E], ones, hot[:, 0:T * E], start=True, stop=True).then_inc(s["cnt_mm"], 1)

            def shared(c, u):
                s = B[0]
                if c == 0:
                    pe.wait_ge(sh["w_in"], 3 * 16)
                    pe.wait_ge(sh["xT_kept"], NC * 16)
                    pe.wait_ge(s["lg_ready"], NC)
                    pe.wait_ge(s["xT_ready"], 2 * NC)
                for m in range(SHB):
                    after(pe, sh["hid"], c * SHB + m - 1)
                    for k in range(KD):
                        last = mm(sgP[m % 2], sh_gate[:, k, m * P:(m + 1) * P], xnT_all[:, k, ds(c * CW, CW)], start=k == 0, stop=k == KD - 1)
                    last.then_inc(sh["gu_mm"], 1)
                    for k in range(KD):
                        last = mm(suP[m % 2], sh_up[:, k, m * P:(m + 1) * P], xnT_all[:, k, ds(c * CW, CW)], start=k == 0, stop=k == KD - 1)
                    last.then_inc(sh["gu_mm"], 1)
                pe.wait_ge(sh["hid"], (c + 1) * SHB)
                after(pe, sh["x"], c)
                for t in range(TC):
                    for k in range(SHB):
                        last = mm(sdP[:, t // 2, (t % 2) * D:(t % 2 + 1) * D], sh_hid[u][:, k, t * P:(t + 1) * P], sh_down[:, k],
                                  start=k == 0, stop=k == SHB - 1)
                last.then_inc(sh["d_mm"], 1)

            def experts(l):
                s, S = B[l], NS[l]
                UB, KW = UPW[l] // P, HK[l]
                if l == 0:
                    pe.wait_ge(sh["hid"], NC * SHB)
                    pe.wait_ge(sh["x"], NC)
                else:
                    pe.wait_ge(s["xT_ready"], 2 * NC)
                    pe.wait_ge(s["lg_ready"], NC)
                pe.wait_ge(s["routed"], 3)
                pe.wait_ge(s["w_lo"], PIECES)

                def experts_of(i, n):
                    digits = pe.value_load(packed[0:1, ds(i, 1)], min_val=0, max_val=NE[l] ** (QUAD + 2) - 1)
                    each = 2 * WCOL[l]
                    return [pe.snap((digits // NE[l] ** k) % NE[l] * each, min_val=0, max_val=(NE[l] - 1) * each) for k in range(n)]

                def weights(e, second, part, lo, n):
                    if l == 0:
                        return wts_flat[:, ds(e + (part * PCOL[0] + second * KD * UPW[0] + lo), n)]
                    return wts_flat[:, ds(e + ((second * 2 + part) * PCOL[1] + lo), n)]

                def may_turn(i, u):
                    pe.wait_ge(s["rows_in"][u], (i // 2 + 1) * 16)
                    after(pe, s["rowsT_ready"], i - 1)

                def turn_rows(i, u):
                    for k in range(KD):
                        last = tr(rowsTP[u][:, k * P:(k + 1) * P], rows[u][:, k * P:(k + 1) * P], ident)
                    last.then_inc(s["xt_mm"], 1)

                def may_multiply(i):
                    pe.wait_ge(s["rowsT_ready"], i + 1)
                    if l == 0:
                        after(pe, s["hid_v"], i - 1)
                    else:
                        after(pe, s["hid_a"], (i - 1) * 2)

                n_first, n_second = UB * len(PASSES) * KD, KW * len(PASSES)

                def first_product(e, u, n):
                    m, (w, x), k = n // (len(PASSES) * KD), PASSES[n // KD % len(PASSES)], n % KD
                    last = mm(upP[u][:, m // (UB // 2), m % (UB // 2) * P:(m % (UB // 2) + 1) * P],
                              weights(e, 0, w, k * UPW[l] + m * P, P), rowsT[u][x][:, k],
                              start=n % (len(PASSES) * KD) == 0, stop=n % (len(PASSES) * KD) == len(PASSES) * KD - 1)
                    if (n + 1) % (n_first // 2) == 0:
                        last.then_inc(s["up_mm"], 1)

                def may_finish(i):
                    after(pe, s["y_ready"], i - 1)
                    pe.wait_ge(s["hidT_ready"], (i + 1) * (4 if l else 2))

                def second_product(e, u, n):
                    k, (w, x) = n // len(PASSES), PASSES[n % len(PASSES)]
                    last = mm(yP[u], hidT[u][x][:, k], weights(e, 1, w, k * D, D), start=n == 0, stop=n == n_second - 1)
                    if n == n_second - 1:
                        last.then_inc(s["dn_mm"], 1)

                def step(i, w):
                    left, u = S - 1 - i if isinstance(i, int) else S, 1 - w % 2
                    first = isinstance(i, int) and i == 0
                    if w == 0:
                        loaded[:] = experts_of(0, QUAD + 1) if first else experts_of(i - 1, min(QUAD, left) + 2)
                    e = loaded[w - 1 if isinstance(i, int) and i < QUAD else w] if not first else None
                    e_next = loaded[w + 1 if isinstance(i, int) and i < QUAD else w + 2] if left > 0 else None
                    if left > 0:
                        may_multiply(i + 1)
                    if left > 1:
                        may_turn(i + 2, 1 - u)
                        turn_rows(i + 2, 1 - u)
                    if first:
                        for n in range(n_first):
                            first_product(e_next, u, n)
                        return
                    may_finish(i - 1)
                    for n in range(n_second):
                        second_product(e, u, n)
                        if left > 0:
                            for m in range(n * n_first // n_second, (n + 1) * n_first // n_second):
                                first_product(e_next, u, m)

                loaded = []
                for i in range(2):
                    may_turn(i, i)
                    turn_rows(i, i)
                may_multiply(0)
                e0 = experts_of(0, 1)[0]
                for n in range(n_first):
                    first_product(e0, 0, n)
                for i in range(QUAD):
                    step(i, i)
                with pe.Fori(1, S // QUAD - 1) as j:
                    for w in range(QUAD):
                        step(j * QUAD + w, w)
                for i in range(S // QUAD * QUAD - QUAD, S):
                    step(i, i % QUAD)
                e_last = experts_of(S - 1, 1)[0]
                may_finish(S - 1)
                for n in range(n_second):
                    second_product(e_last, (S - 1) % 2, n)

            pe.wait_ge(once["inputs_in"], 32)
            for l in range(2):
                project(l)
                attend(l)
                route(l)
                if l == 0:
                    shared(0, 0)
                dispatch(l)
                if l == 0:
                    for c in range(1, NC):
                        shared(c, c % 2)
                experts(l)

        @block.scalar
        def _(act):
            fn = nc.scalar.activation

            def project(l):
                s = B[l]

                def root(c):
                    act.wait_ge(s["var_ready"], c + 1)
                    fn(std[:], var_eps[:], ACT.Sqrt).then_inc(s["sd_ready"], 1)

                def step(c, u):
                    act.wait_ge(s["k_mm"], c + 1)
                    after(act, s["kparts_ready"], c)
                    for m in range(KD):
                        last = fn(kf[:, m], kP[:, m], ACT.Identity, bias=bqk[:, 1, m:m + 1])
                    last.then_inc(s["kf_ready"], 1)
                    act.wait_ge(s["tr_mm"], c + 1)
                    after(act, s["q_mm"], c - 1)
                    fn(xnT[u], trT, ACT.Copy).then_inc(s["xT_ready"], 1)
                    if c + 1 < NC:
                        root(c + 1)
                    act.wait_ge(s["q_mm"], c + 1)
                    after(act, s["qparts_ready"], c)
                    for m in range(KD):
                        last = fn(qf[:, m], qP[:, m], ACT.Identity, bias=bqk[:, 0, m:m + 1])
                    last.then_inc(s["qf_ready"], 1)

                root(0)
                in_chunks(step)

            def attend(l):
                s = B[l]
                KW = KV[l]
                NP = 2 * KW

                def step(i, u):
                    first = isinstance(i, int) and i == 0
                    for p in range(NP):
                        half = p // KW
                        act.wait_ge(s["sc_mm"], i * NP + p + 1)
                        if KW == 1:
                            after(act, s["pv_mm"], 2 * (i - 2) + half + 1)
                            dst = probs[2 * u + half]
                        else:
                            after(act, s["pv_mm"], 2 * (i - 1) + half + 1)
                            dst = probs[p]
                        fn(dst.rearrange("p (b w) -> p b w", b=2), sc[p % 2], ACT.Exp, scale=SCALE).then_inc(s["exp_done"], 1)
                        if p == max(NP - 2, 1) and not first:
                            copy_attention(i - 1)
                    act.wait_ge(s["pv_mm"], 2 * (i + 1))
                    after(act, s["ott_mm"], i)
                    fn(att_raw[:], attP, ACT.Copy).then_inc(s["raw_ready"], 1)

                def copy_attention(i):
                    act.wait_ge(s["at_mm"], i + 1)
                    after(act, s["op_mm"], i)
                    fn(attT[:].rearrange("p k t -> p (k t)"), misc[:, 0:D], ACT.Copy).then_inc(s["atT_ready"], 1)

                act.wait_ge(s["kparts_ready"], NC)
                act.wait_ge(s["qparts_ready"], NC)
                in_all_pairs(act, T, step)
                copy_attention(T - 1)

            def route(l):
                s = B[l]

                def root(c):
                    act.wait_ge(s["var_ready"], NC + c + 1)
                    fn(std[:], var_eps[:], ACT.Sqrt).then_inc(s["sd_ready"], 1)

                def step(c, u):
                    if c + 1 < NC:
                        root(c + 1)
                    act.wait_ge(s["tr_mm"], NC + c + 1)
                    after(act, s["r_mm"], c - 1)
                    if l == 0:
                        after(act, sh["xT_kept"], (c - 1) * 16)
                    fn(xnT[u], trT, ACT.Copy).then_inc(s["xT_ready"], 1)
                    if l:
                        cut_all_high1(c, c + 1)

                if l:
                    act.wait_ge(s["x_att"], T)
                root(0)
                in_chunks(step)

            def make_gates(l):
                s = B[l]
                act.wait_ge(s["routed"], 1)
                if l == 0:
                    fn(gates[:], top[:, :, 0:2], ACT.Sigmoid).then_inc(s["gates_ready"], 1)
                else:
                    fn(gap[:], gap[:], ACT.Exp).then_inc(s["gates_ready"], 1)

            def shared(c, u):
                for m in range(SHB):
                    act.wait_ge(sh["gu_mm"], (c * SHB + m) * 2 + 1)
                    after(act, sh["hid"], c * SHB + m - 1)
                    fn(hid[:, (m % 2) * 512:(m % 2 + 1) * 512], sgP[m % 2], ACT.Silu).then_inc(sh["act"], 1)
                    q = c * SHB + m
                    if q == FREE[0]:
                        act.wait_ge(B[0]["scattered"], 2 * T * 16)
                    cut_high(0, q)

            def cut_high(l, q):
                s = B[l]
                if l == 0:
                    act.wait_ge(s["w_staged"][q % 3], (q // 3 + 1) * 32)
                else:
                    act.wait_ge(s["w_staged"][q % (AHEAD + 1)], (q // (AHEAD + 1) + 1) * 16)
                fn(wts[l][:, ds(q * 2, 1)].rearrange("p o c -> p (o c)"), staged[l][q], ACT.Copy, scale=WS).then_inc(s["w_hi"], 1)

            def cut_all_high1(lo, hi):
                s = B[1]
                for q in range(lo, hi):
                    before = [r for r in range(q) if FREE[1] - 1 - r % AHEAD == q and r < AHEAD + 3]
                    if before:
                        act.wait_ge(s["w_lo"], before[-1] + 1)
                    if q == FREE[1]:
                        act.wait_ge(s["scattered"], 2 * T * 16)
                    cut_high(1, q)

            def row_parts(l, i, u):
                s = B[l]
                act.wait_ge(s["xt_mm"], i + 1)
                after(act, s["up_mm"], 2 * (i - 1))
                fn(rowsT[u][0].rearrange("p k t -> p (k t)"), rowsTP[u], ACT.Copy).then_inc(s["rows_hi"], 1)

            def experts0():
                s, S = B[0], NS[0]

                def step(i, u):
                    if not (isinstance(i, int) and i + 2 >= S):
                        row_parts(0, i + 2, u)
                    if not (isinstance(i, int) and i + 1 >= S):
                        gate(i + 1, 1 - u)

                def gate(i, u):
                    act.wait_ge(s["up_mm"], 2 * i + 1)
                    after(act, s["hid_v"], i - 1)
                    fn(gate_act[u], upP[u][:, 0, 0:D], ACT.Silu, scale=1 / WS).then_inc(s["hid_a"], 1)

                row_parts(0, 0, 0)
                row_parts(0, 1, 1)
                gate(0, 0)
                in_all_pairs(act, S, step)

            def experts1():
                s, S = B[1], NS[1]

                def step(i, u):
                    if not (isinstance(i, int) and i + 2 >= S):
                        row_parts(1, i + 2, u)
                    if not (isinstance(i, int) and i + 1 >= S):
                        hidden(i + 1, 1 - u)

                def hidden(i, u):
                    act.wait_ge(s["b1_in"][u], (i // 2 + 1) * 16)
                    for half in range(2):
                        act.wait_ge(s["up_mm"], 2 * i + half + 1)
                        after(act, s["hidT_ready"], 4 * (i - 1) + 2 * half + 2)
                        for k in range(half * 4, half * 4 + 4):
                            last = fn(hid[:, k * P:(k + 1) * P], upP[u][:, half, (k % 4) * P:(k % 4 + 1) * P], ACT.Relu,
                                      bias=b1_col[u][:, k:k + 1], scale=1 / WS)
                        last.then_inc(s["hid_a"], 1)

                row_parts(1, 0, 0)
                row_parts(1, 1, 1)
                hidden(0, 0)
                in_all_pairs(act, S, step)

            act.wait_ge(B[0]["w_in"], 6 * 16)
            for l in range(2):
                if l:
                    act.wait_ge(B[1]["w_in"], 6 * 16)
                project(l)
                attend(l)
                route(l)
                make_gates(l)
                if l == 0:
                    act.wait_ge(B[0]["x_att"], T)
                    in_chunks(shared)
                    experts0()
                else:
                    cut_all_high1(NC, PIECES)
                    experts1()

        @block.vector
        def _(dve):
            v = nc.vector
            own = [Steps(dve, B[l]["step"]) for l in range(2)]

            def normalise(l, c, u, chain, n, free):
                for t in range(TC):
                    last = v.bn_stats(stats[:, t], x_res[:, ds(c * TC + t, 1)].rearrange("p o d -> p (o d)"))
                chain.then(last)
                for t in range(TC):
                    last = v.bn_aggr(mean_var[:, t], stats[:, t])
                chain.then(last)
                v.tensor_scalar(var_eps[:], mean_var[:, :, 1], EPS, None, ALU.add).then_inc(B[l]["var_ready"], 1)
                dve.wait_ge(B[l]["sd_ready"], n + 1)
                chain.then(v.reciprocal(rstd[:], std[:]))
                free()
                for t in range(TC):
                    last = v.tensor_scalar(xn[u][:, t], x_res[:, ds(c * TC + t, 1)].rearrange("p o d -> p (o d)"),
                                           mean_var[:, t, 0:1], rstd[:, t:t + 1], ALU.subtract, ALU.mult)
                last.then_inc(B[l]["xn_ready"], 1)

            def project(l):
                s = B[l]

                def cut(f, parts, chain, s_ready):
                    chain.then(v.tensor_copy(parts[:, 0], f))
                    chain.then(v.tensor_tensor(rest, f, parts[:, 0], ALU.subtract))
                    chain.then(v.tensor_copy(parts[:, 1], rest))
                    v.tensor_tensor(parts[:, 2], rest, parts[:, 1], ALU.subtract).then_inc(s_ready, 1)

                chain = Steps(dve, s["chunk_step"])

                def prepare(c, u):
                    if l:
                        combine(0, c)
                    normalise(l, c, u, chain, c,
                              lambda: after(dve, s["tr_mm"], c - 1))

                def step(c, u):
                    dve.wait_ge(s["kf_ready"], c + 1)
                    after(dve, s["k_stored"], c * 16)
                    cut(kf, k_parts, chain, s["kparts_ready"])
                    dve.wait_ge(s["v_mm"], c + 1)
                    for t in range(TC):
                        last = v.tensor_tensor(v_all[:, ds(c * TC + t, 1), :, 0:HD].rearrange("p o h d -> p (o h) d"),
                                               vP[:, t // 2, (t % 2) * D:(t % 2 + 1) * D].rearrange("p (h d) -> p h d", h=H),
                                               bvo[:, 0].rearrange("p (h d) -> p h d", h=H), ALU.add)
                    last.then_inc(s["v_ready"], 1)
                    if c + 1 < NC:
                        prepare(c + 1, 1 - u)
                    dve.wait_ge(s["qf_ready"], c + 1)
                    after(dve, s["q_stored"], c * 16)
                    cut(qf, q_parts, chain, s["qparts_ready"])

                prepare(0, 0)
                dve.wait_ge(s["w_in"], 6 * 16)
                dve.wait_ge(s["ones_set"], 1)
                in_chunks(step)

            def attend(l):
                s = B[l]
                KW = KV[l]
                NM = 4 * KW
                HM = H // NM

                def maxima(i, u, lo, hi):
                    after(dve, s["nmt_mm"], i - 1)
                    for m in range(lo, hi):
                        dve.wait_ge(s["max_mm"], i * NM + m + 1)
                        v.tensor_reduce(neg_max[u][:, m * HM:(m + 1) * HM], mx[m % 2].rearrange("p (h k) -> p h k", h=HM),
                                        AX.X, ALU.max, negate=True).then_inc(s["max_read"], 1)

                def keep_maxima(i):
                    dve.wait_ge(s["nmt_mm"], i + 1)
                    after(dve, s["shift_in"], i * 16)
                    v.tensor_copy(neg_maxT[:], misc[0:H, 0:P]).then_inc(s["nm_ready"], 1)

                def divide(i):
                    dve.wait_ge(s["ott_mm"], i + 1)
                    sums = misc.rearrange("p (h c) -> p h c", c=32)
                    v.reciprocal(inv_den[:], sums[:, :, HD:V1]).then_inc(s["norm_step"], 1)
                    dve.wait_ge(s["norm_step"], i + 1)
                    after(dve, s["at_mm"], i)
                    v.tensor_tensor(att[:].rearrange("p (h d) -> p h d", h=H), sums[:, :, 0:HD],
                                    inv_den[:].to_broadcast([P, H, HD]), ALU.mult).then_inc(s["norm_done"], 1)

                def add(i):
                    dve.wait_ge(s["op_mm"], i + 1)
                    x = x_res[:, ds(i, 1)].rearrange("p o d -> p (o d)")
                    v.tensor_tensor(x, misc[:, 0:D], x, ALU.add).then_inc(s["x_att"], 1)

                def step(i, u):
                    first, left = isinstance(i, int) and i == 0, T - 1 - i if isinstance(i, int) else T
                    if left > 0:
                        keep_maxima(i + 1)
                    if left > 1:
                        maxima(i + 2, u, 0, SPREAD[l][1])
                    if not first:
                        divide(i - 1)
                    if left > 1:
                        maxima(i + 2, u, SPREAD[l][1], SPREAD[l][2 * KW + 1])
                    if not first:
                        add(i - 1)
                    if left > 1:
                        maxima(i + 2, u, SPREAD[l][2 * KW + 1], NM)

                dve.wait_ge(s["qf_ready"], NC)
                v.memset(attP, 0.0).then_inc(s["v_ready"], 1)
                dve.wait_ge(s["bo_added"], NC)
                maxima(0, 0, 0, NM)
                keep_maxima(0)
                maxima(1, 1, 0, NM)
                in_all_pairs(dve, T, step)
                divide(T - 1)
                add(T - 1)

            def route(l):
                s, E = B[l], NE[l]

                chain = Steps(dve, s["chunk_step"], NC * 9)

                def prepare(c, u):
                    def free():
                        dve.wait_ge(s["tr_mm"], NC + c - 1)
                        after(dve, s["xn_kept"], (c - 1) * 16)
                    normalise(l, c, u, chain, NC + c, free)

                def step(c, u):
                    if c + 1 < NC:
                        prepare(c + 1, 1 - u)
                    if l:
                        cut_low(1, c)
                    dve.wait_ge(s["r_mm"], c + 1)
                    v.tensor_tensor(logits[:, ds(c * TC, TC), 0:E], rP[u][:, 0:TC * E].rearrange("p (t e) -> p t e", t=TC),
                                    router_b[:, 0:E].rearrange("p (o e) -> p o e", o=1).to_broadcast([P, TC, E]),
                                    ALU.add).then_inc(s["lg_ready"], 1)
                    dve.wait_ge(s["lg_ready"], c + 1)
                    for t in range(c * TC, (c + 1) * TC):
                        last = v.max(top[:, t], logits[:, t, 0:E])
                    chain.then(last)
                    for t in range(c * TC, (c + 1) * TC):
                        last = v.max_index(top_i[:, t], top[:, t], logits[:, t, 0:E])
                    chain.then(last)

                dve.wait_ge(s["x_att"], T)
                prepare(0, 0)
                in_chunks(step)

            def dispatch(l):
                s, E, S = B[l], NE[l], NS[l]
                chain = own[l]
                by_e = lambda x: x.rearrange("p (t o) -> p t o", o=1).to_broadcast([P, T, E])
                over_t = lambda x: x.rearrange("p (o e) -> p o e", o=1).to_broadcast([P, T, E])
                h1, h2, ha, cn, r0, r1 = (x[:, 0:T * E].rearrange("p (t e) -> p t e", t=T)
                                          for x in (hot1, hot2, hot, cnt, run0, run1))

                if l == 0:
                    chain.then(v.tensor_copy(idx_f[:, 0], top_i[:, :, 0:1]))
                    v.tensor_copy(idx_f[:, 1], top_i[:, :, 1:2]).then_inc(s["routed"], 1)
                    dve.wait_ge(s["routed"], 1)
                else:
                    chain.then(v.tensor_copy(idx_f[:, 0], top_i[:, :, 0:1]))
                    chain.then(v.tensor_copy(idx_f[:, 1], top_i[:, :, 1:2]))
                    v.tensor_tensor(gap[:], top[:, :, 1], top[:, :, 0], ALU.subtract).then_inc(s["routed"], 1)
                v.tensor_tensor(h1, over_t(iota_e[:, 0:E]), idx_f[:, 0].to_broadcast([P, T, E]), ALU.is_equal)
                chain.then(v.tensor_tensor(h2, over_t(iota_e[:, 0:E]), idx_f[:, 1].to_broadcast([P, T, E]), ALU.is_equal))
                v.tensor_tensor(ha, h1, h2, ALU.add).then_inc(s["routed"], 1)

                if l == 0:
                    shared(0, 0)
                dve.wait_ge(s["cnt_mm"], 1)
                chain.then(v.tensor_copy(cn, cntP[:, 0:T * E].rearrange("p (t e) -> p t e", t=T)))
                src, dst = cn, r0
                for d in STEPS(T):
                    v.tensor_copy(dst[:, 0:d], src[:, 0:d])
                    chain.then(v.tensor_tensor(dst[:, d:T], src[:, d:T], src[:, 0:T - d], ALU.add))
                    src, dst = dst, (r1 if dst is r0 else r0)
                run, other = src, dst
                chain.then(v.tensor_tensor(over[:, 0:E], run[:, T - 1].rearrange("p (e o) -> p e o", o=1).to_broadcast([P, E, 16]),
                                           iota_c.rearrange("p (o c) -> p o c", o=1).to_broadcast([P, E, 16]), ALU.is_gt))
                chain.then(v.reduce_sum(tiles_e[:, 0:E], over[:, 0:E], axis=AX.X))
                src, dst = tiles_e, end0
                for d in STEPS(E):
                    v.tensor_copy(dst[:, 0:d], src[:, 0:d])
                    chain.then(v.tensor_tensor(dst[:, d:E], src[:, d:E], src[:, 0:E - d], ALU.add))
                    src, dst = dst, (end1 if dst is end0 else end0)
                end = src
                chain.then(v.tensor_tensor(le[:, 0:S, 0:E], end[:, 0:E].rearrange("p (o e) -> p o e", o=1).to_broadcast([P, S, E]),
                                           iota_s[:, 0:S].rearrange("p (s o) -> p s o", o=1).to_broadcast([P, S, E]), ALU.is_le))
                chain.then(v.reduce_sum(exp_f[:, 0:S], le[:, 0:S, 0:E], axis=AX.X))
                chain.then(v.tensor_scalar(exp_f[:, 0:S], exp_f[:, 0:S], float(E - 1), None, ALU.min))
                v.tensor_copy(expert[:, 0:S], exp_f[:, 0:S])
                chain.then(v.tensor_copy(packed_f[:, 0:S], exp_f[:, 0:S]))
                for k in range(1, QUAD + 2):
                    chain.then(v.scalar_tensor_tensor(out=packed_f[:, 0:S - k], in0=exp_f[:, k:S], scalar=float(E ** k),
                                                      in1=packed_f[:, 0:S - k], op0=ALU.mult, op1=ALU.add))
                chain.then(v.tensor_copy(packed[:, 0:S], packed_f[:, 0:S]))
                chain.then(v.tensor_tensor(base[:, 0:E], end[:, 0:E], tiles_e[:, 0:E], ALU.subtract))
                chain.then(v.tensor_scalar(base[:, 0:E], base[:, 0:E], float(P), None, ALU.mult))
                chain.then(v.tensor_tensor(other, run, cn, ALU.subtract))
                chain.then(v.tensor_tensor(other, other, over_t(base[:, 0:E]), ALU.add))
                chain.then(v.tensor_tensor(other, posP[:, 0:T * E].rearrange("p (t e) -> p t e", t=T), other, ALU.add))
                for i, h in enumerate((h1, h2)):
                    chain.then(v.tensor_tensor(cn, h, other, ALU.mult))
                    chain.then(v.reduce_sum(slot_f[:, i], cn, axis=AX.X))
                v.tensor_copy(slot[:], slot_f[:]).then_inc(s["routed"], 1)

                if l == 1:
                    dve.wait_ge(s["gates_ready"], 1)
                    dve.wait_ge(s["routed"], 3)
                    chain.then(v.tensor_scalar(slot_f[:, 0], gap[:], 1.0, None, ALU.add))
                    chain.then(v.reciprocal(gates[:, :, 0], slot_f[:, 0]))
                    chain.then(v.tensor_tensor(gates[:, :, 1], gates[:, :, 0], gap[:], ALU.mult))

            def shared(c, u):
                for m in range(SHB):
                    dve.wait_ge(sh["gu_mm"], (c * SHB + m) * 2 + 2)
                    dve.wait_ge(sh["act"], c * SHB + m + 1)
                    if m == 0:
                        after(dve, sh["d_mm"], c - 1)
                    v.tensor_tensor(sh_hid[u][:, m], suP[m % 2], hid[:, (m % 2) * 512:(m % 2 + 1) * 512], ALU.mult).then_inc(sh["hid"], 1)
                    cut_low(0, c * SHB + m)
                dve.wait_ge(sh["d_mm"], c + 1)
                x = x_res[:, ds(c * TC, TC)].rearrange("p (b t) d -> p b (t d)", b=2)
                v.tensor_tensor(x, sdP, x, ALU.add).then_inc(sh["x"], 1)

            def cut_low(l, q):
                s = B[l]
                dve.wait_ge(s["w_hi"], q + 1)
                high, low = (wts[l][:, ds(q * 2 + part, 1)].rearrange("p o c -> p (o c)") for part in range(2))
                v.scalar_tensor_tensor(out=low, in0=staged[l][q], scalar=WS, in1=high, op0=ALU.mult, op1=ALU.subtract).then_inc(s["w_lo"], 1)

            def row_parts(l, i, u):
                s = B[l]
                dve.wait_ge(s["rows_hi"], i + 1)
                v.tensor_tensor(rowsT[u][1].rearrange("p k t -> p (k t)"), rowsTP[u], rowsT[u][0].rearrange("p k t -> p (k t)"),
                                ALU.subtract).then_inc(s["rowsT_ready"], 1)

            def hidden_parts(l, h, dst, count):
                s = B[l]
                v.tensor_copy(dst[0], h).then_inc(s["hidT_ready"], 1)
                dve.wait_ge(s["hidT_ready"], 2 * count + 1)
                v.tensor_tensor(dst[1], h, dst[0], ALU.subtract).then_inc(s["hidT_ready"], 1)

            def keep_result(l, i, u):
                s = B[l]
                dve.wait_ge(s["dn_mm"], i + 1)
                after(dve, s["y_stored"][u], (i // 2) * 16)
                if l == 0:
                    v.tensor_scalar(y_rows[u], yP[u], 1 / (WS * HS[0]), None, ALU.mult).then_inc(s["y_ready"], 1)
                else:
                    dve.wait_ge(s["b2_in"][u], (i // 2 + 1) * 16)
                    v.scalar_tensor_tensor(out=y_rows[u], in0=yP[u], scalar=1 / (WS * HS[1]), in1=b2_row[u],
                                           op0=ALU.mult, op1=ALU.add).then_inc(s["y_ready"], 1)

            def experts(l):
                s, S = B[l], NS[l]

                def hidden0(i, u):
                    dve.wait_ge(s["up_mm"], 2 * i + 2)
                    dve.wait_ge(s["hid_a"], i + 1)
                    after(dve, s["hidT_ready"], 2 * i)
                    v.scalar_tensor_tensor(out=hid[:, 0:D], in0=upP[u][:, 1, 0:D], scalar=HS[0] / WS, in1=gate_act[u],
                                           op0=ALU.mult, op1=ALU.mult).then_inc(s["hid_v"], 1)
                    dve.wait_ge(s["hid_v"], i + 1)
                    after(dve, s["dn_mm"], i - 1)
                    hidden_parts(0, hid[:, 0:D], [hidT[u][part][:, 0:KD].rearrange("p k t -> p (k t)") for part in range(2)], i)

                def hidden1(i, u):
                    after(dve, s["dn_mm"], i - 1)
                    for half in range(2):
                        dve.wait_ge(s["hid_a"], 2 * i + half + 1)
                        hidden_parts(1, hid[:, half * 512:(half + 1) * 512],
                                     [hidT[u][part][:, half * 4:half * 4 + 4].rearrange("p k t -> p (k t)") for part in range(2)],
                                     2 * i + half)

                hidden = hidden1 if l else hidden0

                def step(i, u):
                    if not (isinstance(i, int) and i + 2 >= S):
                        row_parts(l, i + 2, u)
                    if not (isinstance(i, int) and i < 1):
                        keep_result(l, i - 1, 1 - u)
                    if not (isinstance(i, int) and i + 1 >= S):
                        hidden(i + 1, 1 - u)

                row_parts(l, 0, 0)
                row_parts(l, 1, 1)
                hidden(0, 0)
                in_all_pairs(dve, S, step)
                keep_result(l, S - 1, (S - 1) % 2)

            def combine(l, g):
                s = B[l]
                chain = own[l]
                dve.wait_ge(s["gates_ready"], 1)
                dve.wait_ge(s["gathered"][g % 2], (g // 2 + 1) * 2 * T // GROUPS * 16)
                for i in range(2):
                    for t in range(g * T // GROUPS, (g + 1) * T // GROUPS):
                        last = v.scalar_tensor_tensor(out=x_res[:, t], in0=y_got[:, t, i], scalar=gates[:, t, i:i + 1],
                                                      in1=x_res[:, t], op0=ALU.mult, op1=ALU.add)
                        if i == 1:
                            last.then_inc(s["x_ffn"], 1)
                    if i == 0:
                        chain.then(last)
                dve.wait_ge(s["x_ffn"], (g + 1) * T // GROUPS)

            dve.wait_ge(once["inputs_in"], 32)
            for l in range(2):
                project(l)
                attend(l)
                route(l)
                dispatch(l)
                if l == 0:
                    for c in range(1, NC):
                        shared(c, c % 2)
                else:
                    for q in range(NC, PIECES):
                        cut_low(1, q)
                experts(l)
            for g in range(GROUPS):
                combine(1, g)

        @block.gpsimd
        def _(pool):
            pool.memset(zeros, 0.0).then_inc(once["zeros_set"], 1)
            for l in range(2):
                s = B[l]
                if l == 0:
                    pool.wait_ge(once["zeros_set"], 1)
                    pool.memset(v_all, 1.0).then_inc(s["ones_set"], 1)
                pool.wait_ge(s["w_in"], 6 * 16)

                def add_bias(c, u):
                    pool.wait_ge(s["xn_ready"], c + 1)
                    x = x_res[:, ds(c * TC, TC)]
                    pool.tensor_tensor(x, x, bvo[:, 1:2].to_broadcast([P, TC, D]), ALU.add).then_inc(s["bo_added"], 1)

                in_pairs(pool, NC, add_bias)

                pool.wait_ge(once["slots_zeroed"], T * 16)
                pool.wait_ge(s["xn_kept"], NC * 16)
                pool.wait_ge(s["routed"], 3)
                for t in range(T):
                    for i in range(2):
                        pool.indirect_dma_start(slot_in, bass.IndirectOffsetOnAxis(ap=slot[:, i, t:t + 1], axis=0),
                                                xn_all[l][:, t], None).then_inc(s["scattered"], 16)
                pool.wait_ge(s["scattered"], 2 * T * 16)
                pool.wait_ge(s["w_lo"], PIECES if l == 0 else PIECES - 2)

                def load_rows(i, u):
                    after(pool, s["xt_mm"], i - 1)
                    pool.dma_start(rows[u], slot_in[ds(i * P, P), :]).then_inc(s["rows_in"][u], 16)

                in_all_pairs(pool, NS[l], load_rows)
                for u in range(2):
                    pool.wait_ge(s["y_stored"][u], (NS[l] + 1 - u) // 2 * 16)
                if l == 0:
                    pool.memset(v_all, 1.0).then_inc(B[1]["ones_set"], 1)
                for g in range(GROUPS):
                    after(pool, s["gathered"][g % 2], g // 2 * 2 * T // GROUPS * 16)
                    for t in range(g * T // GROUPS, (g + 1) * T // GROUPS):
                        for i in range(2):
                            pool.indirect_dma_start(y_got[:, t, i], None, slot_out[l],
                                                    bass.IndirectOffsetOnAxis(ap=slot[:, i, t:t + 1], axis=0)).then_inc(s["gathered"][g % 2], 16)


def kernel(**inputs):
    import numpy as np
    import concourse.bacc as bacc
    from concourse import mybir as mb
    from concourse.bass_utils import run_bass_kernel_spmd as run

    g = {k: np.asarray(v) for k, v in inputs.items()}
    shape = g["x"].shape
    d = shape[-1]
    p = 128
    c = np.zeros((p, 3 * p + 32 + 48), np.float32)
    c[:, 0:p] = np.eye(p)
    c[:, p:2 * p] = np.arange(p)[:, None] < np.arange(p)[None, :]
    c[:, 2 * p:3 * p] = 1
    c[:, 3 * p:3 * p + 16] = np.arange(16)
    c[:, 3 * p + 16:3 * p + 32] = p * np.arange(16)
    c[:, 3 * p + 32:] = np.arange(48)
    cols = lambda b: b.reshape(2, p).T
    w0, b0 = g["L0_xattn_in_proj_w"], g["L0_xattn_in_proj_b"]
    arrays = {
        "ones_row": np.full((1, 16384), 0x3F803F80, np.uint32).view(np.float32),
        "x": g["x"].reshape(-1, d), "ctxT": g["ctx_1024"].reshape(-1, d).T, "consts": c,
        "att_w0": np.concatenate([w0[0:d].T, w0[d:2 * d].T, w0[2 * d:].T, g["L0_xattn_out_w"].T]),
        "att_w1": np.concatenate([g[f"L1_xattn_W{n}"].T for n in "qkvo"]),
        "bqk0": np.concatenate([cols(b0[0:d]), cols(b0[d:2 * d])], 1),
        "bqk1": np.concatenate([cols(g["L1_xattn_bq"]), cols(g["L1_xattn_bk"])], 1),
        "bvo0": np.stack([b0[2 * d:], g["L0_xattn_out_b"]]), "bvo1": np.stack([g["L1_xattn_bv"], g["L1_xattn_bo"]]),
        "router_w0": g["L0_ffn_router_w"].T, "router_w1": g["L1_ffn_W_router"],
        "router_b0": np.zeros((1, 16), np.float32), "router_b1": g["L1_ffn_b_router"][None],
        "sh_gate": g["L0_ffn_shared_gate_w"].T, "sh_up": g["L0_ffn_shared_up_w"].T, "sh_down": g["L0_ffn_shared_down_w"].T,
        "exp_up0": g["L0_ffn_gate_up_w"], "exp_dn0": g["L0_ffn_down_w"],
        "exp_up1": g["L1_ffn_W1"], "exp_dn1": g["L1_ffn_W2"],
        "exp_b1": g["L1_ffn_b1"].reshape(8, 8, p).transpose(0, 2, 1), "exp_b2": g["L1_ffn_b2"],
    }
    arrays = {k: np.ascontiguousarray(v) for k, v in arrays.items()}
    nc = bacc.Bacc("TRN2", target_bir_lowering=False, num_devices=1)
    aps = {k: nc.dram_tensor(f"in_{k}", v.shape, mb.dt.from_np(v.dtype), kind="ExternalInput").ap() for k, v in arrays.items()}
    out = nc.dram_tensor("out", (shape[0] * shape[1], d), mb.dt.float32, kind="ExternalOutput").ap()
    xattn_moe_program(nc, aps, out)
    got = run(nc, [{f"in_{k}": v for k, v in arrays.items()}], core_ids=[0]).results[0]["out"]
    return got.reshape(shape)
```
